# Optimizing a Trainium2 kernel written in Bass

```python
import numpy as np
import jax
import jax.numpy as jnp

def _softmax(x, axis=-1):
    return jax.nn.softmax(x, axis=axis)

def _gelu(x):
    return jax.nn.gelu(x, approximate=True)

def _silu(x):
    return jax.nn.silu(x)

def _sigmoid(x):
    return jax.nn.sigmoid(x)

def _layernorm(x, axis=-1, eps=1e-05):
    m = jnp.mean(x, axis=axis, keepdims=True)
    v = jnp.var(x, axis=axis, keepdims=True)
    return (x - m) / jnp.sqrt(v + eps)

def _scatter_add(tgt, idx, src, axis=0):
    return tgt.at[idx].add(src)

def _segment_sum(src, seg, n):
    return jax.ops.segment_sum(src, seg, n)
kernel_name = 'mk_cond_seq_d2_seqx_r4_4558c1'

def setup_inputs(seed: int=0):
    np.random.seed(seed)
    _w = jnp.asarray

    def _rec_inputs():
        import jax
        import jax.numpy as jnp
        _rk = jax.random.key(seed)
        x = 1.648e-05 + 1 * jax.random.normal(jax.random.fold_in(_rk, 1), (8, 256, 256), jnp.float32)
        _lenS = 256 - jax.random.randint(jax.random.fold_in(_rk, 7), (8,), 0, max(1, 256 // 4) + 1, jnp.int32)
        _lenS2 = 256 - jax.random.randint(jax.random.fold_in(_rk, 8), (8,), 0, max(1, 256 // 4) + 1, jnp.int32)
        cond_1024 = 0.00191187 + 0.999416 * jax.random.normal(jax.random.fold_in(_rk, 11), (8, 256), jnp.float32)
        _validS = jnp.arange(256)[None, :] < _lenS[:, None]
        _validS2 = jnp.arange(256)[None, :] < _lenS2[:, None]
        _causal = jnp.tril(jnp.ones((256, 256), dtype=bool))
        mask_BxSxSx11_ik0 = jnp.where(jnp.ones((8, 256, 256, 11), dtype=bool), 0, 1).astype(jnp.int32)
        return (x, cond_1024, mask_BxSxSx11_ik0)
    x, cond_1024, mask_BxSxSx11_ik0 = _rec_inputs()

    def _L0_cond_setup():
        import jax, jax.numpy as jnp
        import numpy as np
        NONGT = 20
        H = 16
        NEG = -9000000000000000.0

        def _gat_attention(self_feat, cond_adj, label_bias, Wq, bq, Wk, bk, Wout, bout):
            B, N, F = self_feat.shape
            ng = min(NONGT, N)
            dh = F // H
            kv = self_feat[:, :ng]
            qh = (self_feat @ Wq.T + bq).reshape(B, N, H, dh)
            kh = (kv @ Wk.T + bk).reshape(B, ng, H, dh)
            aff = jnp.einsum('bnhd,bmhd->bnhm', qh, kh) * (1.0 / np.sqrt(dh))
            mask = cond_adj[:, :, None, :] > 0
            aff = jnp.where(mask, aff, NEG) + label_bias[:, :, None, :]
            w = jax.nn.softmax(aff, axis=-1)
            out_t = jnp.einsum('bnhm,bmf->bnhf', w, kv)
            out = jnp.einsum('bnhf,hgf->bnhg', out_t, Wout) + bout.reshape(H, F // H)
            return out.reshape(B, N, F)

        def _forward(v, q, adj, W_self, b_self, w_bias, b_bias, Wq, bq, Wk, bk, Wout, bout):
            adj_f = adj.astype(jnp.float32)
            exp_v = v
            row_zero = exp_v.sum(-1) == 0
            q_exp = jnp.where(row_zero[..., None], 0.0, q[:, None, :])
            vcq = jnp.concatenate([exp_v, q_exp], axis=-1)
            self_feat = vcq @ W_self.T + b_self
            output = self_feat
            for d in range(2):
                A = adj_f if d == 0 else jnp.swapaxes(adj_f, 1, 2)
                A = A[:, :, :NONGT, :]
                cond = A.sum(-1)
                vb = A @ w_bias + b_bias
                output = output + _gat_attention(self_feat, cond, vb, Wq[d], bq[d], Wk[d], bk[d], Wout[d], bout[d])
            rel = jax.nn.relu(output)
            return exp_v + rel
        key = jax.random.key(seed)
        ks = jax.random.split(key, 8)
        B, N, L, F, Q = (64, 36, 11, 256, 256)
        IN = F + Q
        s = 0.02
        return {'v': jax.random.normal(ks[0], (B, N, F), jnp.float32), 'q': jax.random.normal(ks[1], (B, Q), jnp.float32), 'adj': jax.random.randint(ks[2], (B, N, N, L), 0, 2, jnp.int32), 'W_self': jax.random.normal(ks[3], (F, IN), jnp.float32) * s, 'b_self': jnp.zeros((F,), jnp.float32), 'w_bias': jax.random.normal(ks[4], (L,), jnp.float32) * s, 'b_bias': jnp.zeros((), jnp.float32), 'Wq': jax.random.normal(ks[5], (2, F, F), jnp.float32) * s, 'bq': jnp.zeros((2, F), jnp.float32), 'Wk': jax.random.normal(ks[6], (2, F, F), jnp.float32) * s, 'bk': jnp.zeros((2, F), jnp.float32), 'Wout': jax.random.normal(ks[7], (2, H, F // H, F), jnp.float32) * s, 'bout': jnp.zeros((2, F), jnp.float32)}
    _L0_cond_all = _L0_cond_setup()
    _L0_cond_in = {k: v for k, v in _L0_cond_all.items() if k in ('W_self', 'b_self', 'w_bias', 'b_bias', 'Wq', 'bq', 'Wk', 'bk', 'Wout', 'bout')}
    del _L0_cond_all

    def _L1_cond_setup():
        import jax, jax.numpy as jnp
        import numpy as np
        D_MODEL = 256
        N_HEADS = 16
        HEAD_DIM = D_MODEL // N_HEADS
        D_FF = 1024
        EPS = 1e-05
        THETA = 10000.0
        B, S = (2, 512)

        def _rope_cache(seq_len, head_dim, theta=THETA):
            inv_freq = 1.0 / theta ** (jnp.arange(0, head_dim, 2, dtype=jnp.float32) / head_dim)
            t = jnp.arange(seq_len, dtype=jnp.float32)
            freqs = jnp.einsum('i,j->ij', t, inv_freq)
            emb = jnp.concatenate([freqs, freqs], axis=-1)
            return (jnp.cos(emb), jnp.sin(emb))

        def _rotate_half(x):
            x1, x2 = jnp.split(x, 2, axis=-1)
            return jnp.concatenate([-x2, x1], axis=-1)

        def _ada_rmsnorm(x, time_emb, weight, w1, b1, w2, b2):
            h = jax.nn.silu(time_emb @ w1 + b1)
            scale, shift = jnp.split(h @ w2 + b2, 2, axis=-1)
            norm = x * jax.lax.rsqrt(jnp.mean(x * x, axis=-1, keepdims=True) + EPS)
            return norm * weight * (1.0 + scale[:, None, :]) + shift[:, None, :]
        key = jax.random.key(seed)
        ks = jax.random.split(key, 24)
        rn = lambda k, shp: jax.random.normal(k, shp, dtype=jnp.float32) * 0.02
        return {'x': jax.random.normal(ks[0], (B, S, D_MODEL), dtype=jnp.float32), 'time_emb': jax.random.normal(ks[1], (B, D_MODEL), dtype=jnp.float32), 'w_norm1': jnp.ones((D_MODEL,), jnp.float32), 't1_w1': rn(ks[2], (D_MODEL, D_MODEL)), 't1_b1': jnp.zeros((D_MODEL,), jnp.float32), 't1_w2': rn(ks[3], (D_MODEL, 2 * D_MODEL)), 't1_b2': jnp.zeros((2 * D_MODEL,), jnp.float32), 'w_norm2': jnp.ones((D_MODEL,), jnp.float32), 't2_w1': rn(ks[4], (D_MODEL, D_MODEL)), 't2_b1': jnp.zeros((D_MODEL,), jnp.float32), 't2_w2': rn(ks[5], (D_MODEL, 2 * D_MODEL)), 't2_b2': jnp.zeros((2 * D_MODEL,), jnp.float32), 'wq': rn(ks[6], (D_MODEL, D_MODEL)), 'bq': jnp.zeros((D_MODEL,), jnp.float32), 'wk': rn(ks[7], (D_MODEL, D_MODEL)), 'bk': jnp.zeros((D_MODEL,), jnp.float32), 'wv': rn(ks[8], (D_MODEL, D_MODEL)), 'bv': jnp.zeros((D_MODEL,), jnp.float32), 'wo': rn(ks[9], (D_MODEL, D_MODEL)), 'bo': jnp.zeros((D_MODEL,), jnp.float32), 'w_gate': rn(ks[10], (D_MODEL, D_FF)), 'w_up': rn(ks[11], (D_MODEL, D_FF)), 'w_down': rn(ks[12], (D_FF, D_MODEL))}
    _L1_cond_all = _L1_cond_setup()
    _L1_cond_in = {k: v for k, v in _L1_cond_all.items() if k in ('w_norm1', 't1_w1', 't1_b1', 't1_w2', 't1_b2', 'w_norm2', 't2_w1', 't2_b1', 't2_w2', 't2_b2', 'wq', 'bq', 'wk', 'bk', 'wv', 'bv', 'wo', 'bo', 'w_gate', 'w_up', 'w_down')}
    del _L1_cond_all
    return {'x': x, 'cond_1024': cond_1024, 'mask_BxSxSx11_ik0': mask_BxSxSx11_ik0, 'L0_cond_W_self': _L0_cond_in['W_self'], 'L0_cond_b_self': _L0_cond_in['b_self'], 'L0_cond_w_bias': _L0_cond_in['w_bias'], 'L0_cond_b_bias': _L0_cond_in['b_bias'], 'L0_cond_Wq': _L0_cond_in['Wq'], 'L0_cond_bq': _L0_cond_in['bq'], 'L0_cond_Wk': _L0_cond_in['Wk'], 'L0_cond_bk': _L0_cond_in['bk'], 'L0_cond_Wout': _L0_cond_in['Wout'], 'L0_cond_bout': _L0_cond_in['bout'], 'L1_cond_w_norm1': _L1_cond_in['w_norm1'], 'L1_cond_t1_w1': _L1_cond_in['t1_w1'], 'L1_cond_t1_b1': _L1_cond_in['t1_b1'], 'L1_cond_t1_w2': _L1_cond_in['t1_w2'], 'L1_cond_t1_b2': _L1_cond_in['t1_b2'], 'L1_cond_w_norm2': _L1_cond_in['w_norm2'], 'L1_cond_t2_w1': _L1_cond_in['t2_w1'], 'L1_cond_t2_b1': _L1_cond_in['t2_b1'], 'L1_cond_t2_w2': _L1_cond_in['t2_w2'], 'L1_cond_t2_b2': _L1_cond_in['t2_b2'], 'L1_cond_wq': _L1_cond_in['wq'], 'L1_cond_bq': _L1_cond_in['bq'], 'L1_cond_wk': _L1_cond_in['wk'], 'L1_cond_bk': _L1_cond_in['bk'], 'L1_cond_wv': _L1_cond_in['wv'], 'L1_cond_bv': _L1_cond_in['bv'], 'L1_cond_wo': _L1_cond_in['wo'], 'L1_cond_bo': _L1_cond_in['bo'], 'L1_cond_w_gate': _L1_cond_in['w_gate'], 'L1_cond_w_up': _L1_cond_in['w_up'], 'L1_cond_w_down': _L1_cond_in['w_down']}

def reference(x, cond_1024, mask_BxSxSx11_ik0, L0_cond_W_self, L0_cond_b_self, L0_cond_w_bias, L0_cond_b_bias, L0_cond_Wq, L0_cond_bq, L0_cond_Wk, L0_cond_bk, L0_cond_Wout, L0_cond_bout, L1_cond_w_norm1, L1_cond_t1_w1, L1_cond_t1_b1, L1_cond_t1_w2, L1_cond_t1_b2, L1_cond_w_norm2, L1_cond_t2_w1, L1_cond_t2_b1, L1_cond_t2_w2, L1_cond_t2_b2, L1_cond_wq, L1_cond_bq, L1_cond_wk, L1_cond_bk, L1_cond_wv, L1_cond_bv, L1_cond_wo, L1_cond_bo, L1_cond_w_gate, L1_cond_w_up, L1_cond_w_down):
    import jax
    import jax.numpy as jnp

    def _L0_cond_ref(v, q, adj, W_self, b_self, w_bias, b_bias, Wq, bq, Wk, bk, Wout, bout):
        import jax, jax.numpy as jnp
        import numpy as np
        NONGT = 20
        H = 16
        NEG = -9000000000000000.0

        def _gat_attention(self_feat, cond_adj, label_bias, Wq, bq, Wk, bk, Wout, bout):
            B, N, F = self_feat.shape
            ng = min(NONGT, N)
            dh = F // H
            kv = self_feat[:, :ng]
            qh = (self_feat @ Wq.T + bq).reshape(B, N, H, dh)
            kh = (kv @ Wk.T + bk).reshape(B, ng, H, dh)
            aff = jnp.einsum('bnhd,bmhd->bnhm', qh, kh) * (1.0 / np.sqrt(dh))
            mask = cond_adj[:, :, None, :] > 0
            aff = jnp.where(mask, aff, NEG) + label_bias[:, :, None, :]
            w = jax.nn.softmax(aff, axis=-1)
            out_t = jnp.einsum('bnhm,bmf->bnhf', w, kv)
            out = jnp.einsum('bnhf,hgf->bnhg', out_t, Wout) + bout.reshape(H, F // H)
            return out.reshape(B, N, F)

        def _forward(v, q, adj, W_self, b_self, w_bias, b_bias, Wq, bq, Wk, bk, Wout, bout):
            adj_f = adj.astype(jnp.float32)
            exp_v = v
            row_zero = exp_v.sum(-1) == 0
            q_exp = jnp.where(row_zero[..., None], 0.0, q[:, None, :])
            vcq = jnp.concatenate([exp_v, q_exp], axis=-1)
            self_feat = vcq @ W_self.T + b_self
            output = self_feat
            for d in range(2):
                A = adj_f if d == 0 else jnp.swapaxes(adj_f, 1, 2)
                A = A[:, :, :NONGT, :]
                cond = A.sum(-1)
                vb = A @ w_bias + b_bias
                output = output + _gat_attention(self_feat, cond, vb, Wq[d], bq[d], Wk[d], bk[d], Wout[d], bout[d])
            rel = jax.nn.relu(output)
            return exp_v + rel
        return _forward(v, q, adj, W_self, b_self, w_bias, b_bias, Wq, bq, Wk, bk, Wout, bout)

    def _L1_cond_ref(x, time_emb, w_norm1, t1_w1, t1_b1, t1_w2, t1_b2, w_norm2, t2_w1, t2_b1, t2_w2, t2_b2, wq, bq, wk, bk, wv, bv, wo, bo, w_gate, w_up, w_down):
        import jax, jax.numpy as jnp
        import numpy as np
        D_MODEL = 256
        N_HEADS = 16
        HEAD_DIM = D_MODEL // N_HEADS
        D_FF = 1024
        EPS = 1e-05
        THETA = 10000.0
        B, S = (2, 512)

        def _rope_cache(seq_len, head_dim, theta=THETA):
            inv_freq = 1.0 / theta ** (jnp.arange(0, head_dim, 2, dtype=jnp.float32) / head_dim)
            t = jnp.arange(seq_len, dtype=jnp.float32)
            freqs = jnp.einsum('i,j->ij', t, inv_freq)
            emb = jnp.concatenate([freqs, freqs], axis=-1)
            return (jnp.cos(emb), jnp.sin(emb))

        def _rotate_half(x):
            x1, x2 = jnp.split(x, 2, axis=-1)
            return jnp.concatenate([-x2, x1], axis=-1)

        def _ada_rmsnorm(x, time_emb, weight, w1, b1, w2, b2):
            h = jax.nn.silu(time_emb @ w1 + b1)
            scale, shift = jnp.split(h @ w2 + b2, 2, axis=-1)
            norm = x * jax.lax.rsqrt(jnp.mean(x * x, axis=-1, keepdims=True) + EPS)
            return norm * weight * (1.0 + scale[:, None, :]) + shift[:, None, :]
        b, s, _ = x.shape
        cos, sin = _rope_cache(s, HEAD_DIM)
        nx = _ada_rmsnorm(x, time_emb, w_norm1, t1_w1, t1_b1, t1_w2, t1_b2)
        q = (nx @ wq + bq).reshape(b, s, N_HEADS, HEAD_DIM)
        k = (nx @ wk + bk).reshape(b, s, N_HEADS, HEAD_DIM)
        v = (nx @ wv + bv).reshape(b, s, N_HEADS, HEAD_DIM)
        c = cos[:, None, :]
        si = sin[:, None, :]
        q = q * c + _rotate_half(q) * si
        k = k * c + _rotate_half(k) * si
        scores = jnp.einsum('bshd,bthd->bhst', q, k) / jnp.sqrt(jnp.float32(HEAD_DIM))
        probs = jax.nn.softmax(scores, axis=-1)
        attn = jnp.einsum('bhst,bthd->bshd', probs, v).reshape(b, s, D_MODEL)
        x = x + attn @ wo + bo
        nx = _ada_rmsnorm(x, time_emb, w_norm2, t2_w1, t2_b1, t2_w2, t2_b2)
        gate = jax.nn.gelu(nx @ w_gate, approximate=False)
        ff = gate * (nx @ w_up) @ w_down
        return x + ff
    x = _L0_cond_ref(x, cond_1024, mask_BxSxSx11_ik0, L0_cond_W_self, L0_cond_b_self, L0_cond_w_bias, L0_cond_b_bias, L0_cond_Wq, L0_cond_bq, L0_cond_Wk, L0_cond_bk, L0_cond_Wout, L0_cond_bout)
    x = _L1_cond_ref(x, cond_1024, L1_cond_w_norm1, L1_cond_t1_w1, L1_cond_t1_b1, L1_cond_t1_w2, L1_cond_t1_b2, L1_cond_w_norm2, L1_cond_t2_w1, L1_cond_t2_b1, L1_cond_t2_w2, L1_cond_t2_b2, L1_cond_wq, L1_cond_bq, L1_cond_wk, L1_cond_bk, L1_cond_wv, L1_cond_bv, L1_cond_wo, L1_cond_bo, L1_cond_w_gate, L1_cond_w_up, L1_cond_w_down)
    return x

_drawn_inputs = setup_inputs


def setup_inputs(seed=0):
    import zlib

    import numpy as np

    out = dict(_drawn_inputs(seed))
    spreads = {'L0_cond_b_self': (0.0, 0.1),
     'L0_cond_bq': (0.0, 0.1),
     'L0_cond_bk': (0.0, 0.1),
     'L0_cond_bout': (0.0, 0.1),
     'L1_cond_w_norm1': (1.0, 0.6),
     'L1_cond_t1_b1': (0.0, 0.8),
     'L1_cond_t1_b2': (0.0, 0.778),
     'L1_cond_w_norm2': (1.0, 0.6),
     'L1_cond_t2_b1': (0.0, 0.8),
     'L1_cond_t2_b2': (0.0, 0.8),
     'L1_cond_bq': (0.0, 0.8),
     'L1_cond_bk': (0.0, 0.8),
     'L1_cond_bv': (0.0, 0.277),
     'L1_cond_bo': (0.0, 0.1)}
    factors = {'L1_cond_t1_w1': 8.0,
     'L1_cond_t1_w2': 8.0,
     'L1_cond_t2_w1': 8.0,
     'L1_cond_t2_w2': 8.0,
     'L1_cond_wq': 8.0,
     'L1_cond_wk': 8.0}
    for name, (base, spread) in spreads.items():
        noise = np.random.default_rng([zlib.crc32(name.encode()), seed]).standard_normal(out[name].shape)
        drawn = base * np.exp(spread * noise) if base else spread * noise
        out[name] = jnp.asarray(drawn.astype(out[name].dtype))
    for name, factor in factors.items():
        out[name] = (out[name] * factor).astype(out[name].dtype)
    return out
```

```python
import math
from contextlib import ExitStack

import concourse.bass as bass
import concourse.mybir as mybir

FP32 = mybir.dt.float32
F32R = mybir.dt.float32r
INT32 = mybir.dt.int32
ALU = mybir.AluOpType
ACT = mybir.ActivationFunctionType
AX = mybir.AxisListType

P = 128
B, S, D = 8, 256, 256
L = 11
M = 20
MP = 32
H, DH = 16, 16
FF = 1024
EPS = 1e-5
NEG = -9000000000000000.0
SCALE = 1.0 / math.sqrt(DH)
KC = D // P
TC = S // P
PAIRS = H // 2
NFF = FF // P
NJ = NFF // 2
AQ = 4
AN = S // AQ

W_SELF, W_Q0, W_QK, W_V, W_O, W_G, W_U, W_D = 0, 512, 1536, 2560, 3072, 3584, 5632, 7680
W_ALL = 9728
STAGE = 1024
V_BQ0, V_BK0, V_BOUT, V_BV, V_B1, V_B2, V_WN, V_BQK, V_BQKS, V_ALL = 0, 4, 8, 12, 14, 18, 26, 30, 34, 38
C_Q, C_W1, C_W2, C_ALL = 0, 512, 1536, 3584


class Signal:

    def __init__(self, sem, per):
        self.sem, self.per = sem, per

    def wait(self, eng, b, n=None):
        value = b * self.per + (self.per if n is None else n)
        if isinstance(value, int) and value <= 0:
            return
        eng.wait_ge(self.sem, value)


def build(nc, x, adj, condT, wall, wsmall, wcond, cols, rows_in, tabs, out):
    ctx = ExitStack()
    with ctx:
        def sb(name, shape, dt=FP32):
            return ctx.enter_context(nc.sbuf_tensor(name, shape, dt))

        def sig(name, per=1):
            return Signal(ctx.enter_context(nc.semaphore(name)), per)

        wh, wl = sb("wh", [P, W_ALL], F32R), sb("wl", [P, W_ALL], F32R)
        wsm = sb("wsm", [P, 2, 2, KC, D])
        kst = sb("kst", [P, H, S], F32R)
        qst = sb("qst", [P, PAIRS, S], F32R)
        rbT = sb("rbT", [P, 2 * KC, S])
        vec = sb("vec", [P, V_ALL])
        bo = sb("bo", [P, D])
        wb = sb("wb", [P, L + 1])
        rope = sb("rope", [P, 2, TC, DH])
        ident = sb("ident", [P, P])
        sel = sb("sel", [AQ * M, 2, 2, M])
        mask8 = sb("mask8", [P, 8])
        mask4 = sb("mask4", [P, 4])
        mhalf = sb("mhalf", [P, TC])
        cT = sb("cT", [P, KC, B])
        hT = sb("hT", [P, 2, KC, B])
        tab = sb("tab", [P, 2, B, 4])
        cur1, cur2 = sb("cur1", [P, 4]), sb("cur2", [P, 4])
        x_tok = sb("x_tok", [P, TC, D])
        adjR = sb("adjR", [P, TC * M * L], INT32)
        adjC = sb("adjC", [AQ * M, AN * L], INT32)
        cw = sb("cw", [P, 2, 2, TC, M])
        cwC = sb("cwC", [AQ * M, 2, AN])
        msk = sb("msk", [P, 2, TC, M])
        off = sb("off", [P, 2, TC, M])
        rs = sb("rs", [P, TC])
        nz4 = sb("nz4", [P, TC, 4])
        nzT = sb("nzT", [4, S], F32R)
        q4 = sb("q4", [4, D], F32R)
        splx = sb("splx", [P, 2, KC, S], F32R)
        self32 = sb("self32", [P, KC, S])
        kvr = sb("kvr", [P, KC, 4, MP])
        aff = sb("aff", [P, TC, 2, H, M])
        amx = sb("amx", [P, TC, 2 * H])
        asum = sb("asum", [P, TC, 2 * H])
        arc = sb("arc", [P, TC, 2 * H])
        prob = sb("prob", [P, 2 * H, MP])
        vblk = sb("vblk", [P, 2, 4, 64])
        l0 = sb("l0", [P, 2048])
        q0T = l0[:, 0:1024].rearrange("p (d k s) -> p d k s", d=2, k=KC)
        kblk = l0[:, 1024:1664].rearrange("p (d k h m) -> p d k h m", d=2, k=KC, h=8)
        pT = l0[:, :].rearrange("p (d g s) -> p d g s", d=2, g=4)
        yT = l0[:, 0:512].rearrange("p (k s) -> p k s", k=KC)
        prodC = aff[0:AQ * M].rearrange("p c d h m -> p (c d h m)")[:, 0:AN * L]
        prodR = aff[:].rearrange("p c d h m -> p (c d h m)")[:, AN * L:AN * L + TC * M * L]
        x1 = sb("x1", [P, TC, D])
        ss1, v1, r1 = sb("ss1", [P, TC]), sb("v1", [P, TC]), sb("r1", [P, TC])
        sply = sb("sply", [P, 2, KC, S], F32R)
        vv = sb("vv", [P, TC, H, 32])
        nm = sb("nm", [P, TC, H])
        nm4 = sb("nm4", [P, TC, 2, 2, PAIRS], F32R)
        nrow = sb("nrow", [4 * PAIRS, S], F32R)
        orc = sb("orc", [P, TC, H])
        ya = sb("ya", [P, 5632])
        xr = ya[:, 0:512].rearrange("p (c d) -> p c d", c=TC)
        nx32 = ya[:, 512:1024].rearrange("p (k s) -> p k s", k=KC)
        t1 = ya[:, 1024:2048].rearrange("p (c n) -> p c n", c=TC)
        t2 = ya[:, 2048:3072].rearrange("p (c n) -> p c n", c=TC)
        qk32 = ya[:, 3072:3584].rearrange("p (k s) -> p k s", k=KC)
        qkh = ya[:, 3584:4608].rearrange("p (k s) -> p k s", k=2 * KC)
        qkl = ya[:, 4608:5632].rearrange("p (k s) -> p k s", k=2 * KC)
        ex = ya[:, 0:4096].rearrange("p (h c s) -> p h c s", h=8, c=TC)
        oT32 = ya[:, 4096:5120].rearrange("p (g s) -> p g s", g=4)
        attn = ya[:, 5120:5632].rearrange("p (c d) -> p c d", c=TC)
        wc = ya[:, 0:C_ALL]
        stage = ya[:, C_ALL:C_ALL + 2 * STAGE].rearrange("p (n w) -> p n w", n=2)
        a32 = ya[:, 0:512].rearrange("p (k s) -> p k s", k=KC)
        x1b, x2 = sb("x1b", [P, TC, D]), sb("x2", [P, TC, D])
        xr2 = sb("xr2", [P, TC, D])
        res = xr2
        ss2, v2, r2 = sb("ss2", [P, TC]), sb("v2", [P, TC]), sb("r2", [P, TC])
        splz = sb("splz", [P, 2, KC, S], F32R)
        spla = splz
        g32 = sb("g32", [P, 2, 2, S])
        nz32 = g32[:, 0]
        hs = sb("hs", [P, 2, 2, 2, S], F32R)
        qrow = hs[0:B, 0].rearrange("p a i s -> p (a i) s")
        q32, b32 = g32[0:B, 0, 0, :], g32[0:B, 0, 1, :]

        q4_d = nc.dram_tensor("q4_d", [B, 4, D], FP32, kind="Internal").ap()
        qk_d = nc.dram_tensor("qk_d", [2, 2 * D, S], FP32, kind="Internal").ap()

        ps = ctx.enter_context(nc.psum_tensor("ps", [P, 8, 512], FP32))

        x_in, adj_in, q4_in = sig("x_in", 16), sig("adj_in", 32), sig("q4_in", 16)
        vec_in, wsm_in, wc_in, wc2_in = sig("vec_in"), sig("wsm_in"), sig("wc_in"), sig("wc2_in")
        stage_in = [sig("stage_in0"), sig("stage_in1")]
        wsplit = sig("wsplit")
        q4_out = sig("q4_out")
        hi_out, lo_out, stack_in, nrow_in, res_out = (
            sig("hi_out", 16), sig("lo_out", 16), sig("stack_in", 9 * 16), sig("nrow_in", 4 * 16), sig("res_out", 16))
        ident_ok, consts_ok, zero_ok, build_ok = sig("ident_ok"), sig("consts_ok"), sig("zero_ok"), sig("build_ok")
        c_ps, c_sb, h_ok, rb_ok, tab_ok, qrow_ok, bout_ok = (
            sig("c_ps"), sig("c_sb"), sig("h_ok"), sig("rb_ok"), sig("tab_ok"), sig("qrow_ok"), sig("bout_ok"))
        xT_ps, nzT_ps, self_ps, adjT_ps, q0_ps, k0_ps, v0_ps = (
            sig("xT_ps"), sig("nzT_ps"), sig("self_ps"), sig("adjT_ps"), sig("q0_ps", 2), sig("k0_ps"), sig("v0_ps"))
        aff_ps, pT_ps, y_ps, x1_ps = sig("aff_ps", TC), sig("pT_ps", 2 * TC), sig("y_ps"), sig("x1_ps")
        nx_ps, qk_ps, v_ps, qkT_ps, s_ps, nmT_ps, st_ps, pv_ps, oT_ps, aT_ps = (
            sig("nx_ps"), sig("qk_ps", TC), sig("v_ps"), sig("qkT_ps", 2), sig("s_ps", H), sig("nmT_ps"), sig("st_ps", H),
            sig("pv_ps", 4), sig("oT_ps", TC), sig("aT_ps"))
        wo_ps, nz_ps, g_ps, u_ps, d_ps = sig("wo_ps"), sig("nz_ps"), sig("g_ps", NJ), sig("u_ps", NJ), sig("d_ps", NJ)
        rs_ok, nz_ok, nzT_ok, xh_ok, xl_ok, self_ok, selfh_ok, selfl_ok, kvr_ok = (
            sig("rs_ok"), sig("nz_ok"), sig("nzT_ok"), sig("xh_ok"), sig("xl_ok"), sig("self_ok"), sig("selfh_ok"),
            sig("selfl_ok"), sig("kvr_ok"))
        prod_ok, adj_ok, cw_ok, off_ok, msk_ok = sig("prod_ok"), sig("adj_ok"), sig("cw_ok"), sig("off_ok"), sig("msk_ok")
        q0T_ok, kblk_ok, vblk_ok = sig("q0T_ok", 2), sig("kblk_ok"), sig("vblk_ok")
        am_ok, aa_ok, amx_ok, asub_ok, aexp_ok, asum_ok, arc_ok, prob_ok, pT_ok = (
            sig("am_ok", TC), sig("aa_ok", TC), sig("amx_ok", TC), sig("asub_ok", TC), sig("aexp_ok", TC),
            sig("asum_ok", TC), sig("arc_ok", TC), sig("prob_ok", TC), sig("pT_ok", 2 * TC))
        y_ok, yr_ok, x1_ok = sig("y_ok"), sig("yr_ok"), sig("x1_ok")
        cur1_ok, ss1_ok, v1_ok, r1_ok, xr_ok, nx_ok, nxh_ok, nxl_ok = (
            sig("cur1_ok"), sig("ss1_ok", TC), sig("v1_ok"), sig("r1_ok"), sig("xr_ok"), sig("nx_ok"), sig("nxh_ok"), sig("nxl_ok"))
        rot_ok, radd_ok, vv_ok, qk_ok, qkh_ok, qkl_ok = (
            sig("rot_ok", TC), sig("radd_ok", TC), sig("vv_ok"), sig("qk_ok", 2), sig("qkh_ok", 2), sig("qkl_ok", 2))
        mx_ok, nmh_ok, nm4_ok, nrow_ok, ex_ok, o_ok, orc_ok, at_ok, a_ok, ah_ok, al_ok = (
            sig("mx_ok", H), sig("nmh_ok"), sig("nm4_ok"), sig("nrow_ok"), sig("ex_ok", H), sig("o_ok", 2), sig("orc_ok", TC),
            sig("at_ok", TC), sig("a_ok"), sig("ah_ok"), sig("al_ok"))
        x1b_ok, x2_ok, cur2_ok, ss2_ok, v2_ok, r2_ok, xr2_ok, nz_sb, nzh_ok, nzl_ok = (
            sig("x1b_ok"), sig("x2_ok"), sig("cur2_ok"), sig("ss2_ok", TC), sig("v2_ok"), sig("r2_ok"), sig("xr2_ok"),
            sig("nz_sb"), sig("nzh_ok"), sig("nzl_ok"))
        gelu_ok, hm_ok, hh_ok, hl_ok, res_ok = sig("gelu_ok", NJ), sig("hm_ok", NJ), sig("hh_ok", NJ), sig("hl_ok", NJ), sig("res_ok")

        X_USES = [("xT", 3, xl_ok, 1), ("nzT", 4, nzT_ok, 1), ("self", 3, self_ok, 1), ("adjT", 4, cw_ok, 1),
                  ("q0.0", 3, q0T_ok, 1), ("q0.1", 4, q0T_ok, 2), ("k0", 3, kblk_ok, 1),
                  ("aff.0", 3, am_ok, 1), ("aff.0'", 4, am_ok, 1), ("aff.1", 3, am_ok, 2), ("aff.1'", 4, am_ok, 2),
                  ("v0", 3, vblk_ok, 1),
                  ("pT.0", 4, pT_ok, 1), ("pT.1", 3, pT_ok, 2), ("pT.2", 4, pT_ok, 3), ("pT.3", 3, pT_ok, 4),
                  ("y", 4, y_ok, 1), ("x1", 3, x1_ok, 1)]
        Y_USES = ([("nx", 2, nx_ok, 1), ("qk.0", 0, rot_ok, 1), ("qk.1", 1, rot_ok, 2), ("v", 2, vv_ok, 1),
                   ("qkT.0", 0, qk_ok, 1), ("qkT.1", 1, qk_ok, 2)]
                  + [(f"s.{h}", h % 2, mx_ok, h + 1) for h in range(H)] + [("nmT", 2, nrow_ok, 1)]
                  + [(f"st.{h}", h % 2, ex_ok, h + 1) for h in range(H)]
                  + [("o.0", 2, o_ok, 1), ("o.1", 2, o_ok, 2), ("oT.0", 0, at_ok, 1), ("oT.1", 1, at_ok, 2), ("aT", 2, a_ok, 1)])
        Z_USES = ([("wo", 5, x2_ok, 1), ("nz", 6, nz_sb, 1)]
                  + [u for j in range(NJ) for u in ((f"g.{j}", 5, gelu_ok, j + 1), (f"u.{j}", 6, hm_ok, j + 1))]
                  + [("d", 7, res_ok, 1)])
        BANK = {name: bank for uses in (X_USES, Y_USES, Z_USES) for name, bank, _, _ in uses}

        def bank_free(pe, uses, name, b):
            at = [u[0] for u in uses].index(name)
            for back in range(1, len(uses) + 1):
                _, bank, signal, n = uses[(at - back) % len(uses)]
                if bank == BANK[name]:
                    if back <= at:
                        signal.wait(pe, b, n)
                    elif not (isinstance(b, int) and b == 0):
                        signal.wait(pe, b - 1, n)
                    return BANK[name]

        def first(b):
            return isinstance(b, int) and b == 0

        def prev(signal, eng, b, n=None):
            if not first(b):
                signal.wait(eng, b - 1, n)

        block = ctx.enter_context(nc.Block())
        NSTAGE = math.ceil(W_ALL / STAGE)
        staged = [(n * STAGE, min((n + 1) * STAGE, W_ALL)) for n in range(NSTAGE)]

        LEAD = {"X": 1, "Y": 0, "Z": -1}

        def run(eng, steps, order):
            plan = []
            for entry in order.split():
                name, shift = (entry[:-2], int(entry[-2:])) if entry[-2] in "+-" else (entry, 0)
                plan.append((steps[name], LEAD[name[0]] + shift))
            assert len(plan) == len(steps)
            lead, lag = max(o for _, o in plan), min(o for _, o in plan)

            def round_(it):
                for step, o in plan:
                    if not isinstance(it, int) or 0 <= it + o < B:
                        step(it + o)

            for it in range(-lead, 1 - lag):
                round_(it)
            with eng.Fori(1 - lag, B - lead) as it:
                round_(it)
            for it in range(B - lead, B - lag):
                round_(it)

        @block.sync
        def _(sp):
            sp.dma_start(x_tok[:], x[0].rearrange("(c p) d -> p c d", p=P)).then_inc(x_in.sem, 16)
            sp.dma_start(vec[:], cols).then_inc(vec_in.sem, 16)
            sp.dma_start(rope[:], tabs[:, 0:2 * TC * DH].rearrange("p (a c d) -> p a c d", a=2, c=TC)).then_inc(vec_in.sem, 16)
            sp.dma_start(cT[:], condT.rearrange("p (k b) -> p k b", k=KC)).then_inc(vec_in.sem, 16)
            sp.dma_start(bo[:], rows_in[0:1, 0:D].broadcast_to([P, D])).then_inc(vec_in.sem, 16)
            sp.dma_start(wb[:], rows_in[0:1, 2 * D:2 * D + L + 1].broadcast_to([P, L + 1])).then_inc(vec_in.sem, 16)
            sp.dma_start(b32, rows_in[0:1, D:2 * D].broadcast_to([B, D])).then_inc(vec_in.sem, 16)
            sp.dma_start(rbT[:, 0:2, :], tabs[:, 2 * TC * DH:].rearrange("p (a s) -> p a s", a=2)).then_inc(vec_in.sem, 16)
            sp.dma_start(wc[:, 0:C_W1], wcond[:, 0:C_W1]).then_inc(wc_in.sem, 16)
            for n, (a, z) in enumerate(staged):
                if n >= 2:
                    sp.wait_ge(wsplit.sem, 2 * (n - 1))
                sp.dma_start(stage[:, n % 2, 0:z - a], wall[:, a:z]).then_inc(stage_in[n % 2].sem, 16)
                if n == 0:
                    sp.dma_start(adjR[:].rearrange("p (c n) -> p c n", c=TC),
                                 adj[0, :, 0:M, :].rearrange("(c p) m l -> p c (m l)", p=P)).then_inc(adj_in.sem, 16)
                    sp.dma_start(adjC[:], adj[0, 0:M].rearrange("m (q n) l -> (m q) (n l)", q=AQ)).then_inc(adj_in.sem, 16)
                if n == 1:
                    sp.dma_start(wsm[:].rearrange("p a d k n -> p (a d k n)"), wsmall).then_inc(wsm_in.sem, 16)
                    sp.dma_start(wc[:, C_W1:], wcond[:, C_W1:]).then_inc(wc2_in.sem, 16)
                    sp.wait_ge(qrow_ok.sem, 1)
                    sp.dma_start(q4_d.rearrange("b r n -> b (r n)"), qrow.rearrange("b r n -> b (r n)").bitcast(FP32)).then_inc(q4_out.sem, 16)
                    sp.wait_ge(q4_out.sem, 16)
                    sp.dma_start(q4[:].bitcast(FP32), q4_d[0]).then_inc(q4_in.sem, 16)

            def load(b):
                if first(b):
                    return
                prev(self_ps, sp, b)
                sp.dma_start(q4[:].bitcast(FP32), q4_d[b]).then_inc(q4_in.sem, 16)
                prev(adj_ok, sp, b)
                sp.dma_start(adjR[:].rearrange("p (c n) -> p c n", c=TC),
                             adj[b, :, 0:M, :].rearrange("(c p) m l -> p c (m l)", p=P)).then_inc(adj_in.sem, 16)
                sp.dma_start(adjC[:], adj[b, 0:M].rearrange("m (q n) l -> (m q) (n l)", q=AQ)).then_inc(adj_in.sem, 16)
                prev(x1_ok, sp, b)
                sp.dma_start(x_tok[:], x[b].rearrange("(c p) d -> p c d", p=P)).then_inc(x_in.sem, 16)

            def stack(b):
                prev(stack_in, sp, b)
                qkh_ok.wait(sp, b)
                sp.dma_start(qk_d[0].rearrange("(k p) s -> p k s", p=P), qkh).then_inc(hi_out.sem, 16)
                qkl_ok.wait(sp, b)
                sp.dma_start(qk_d[1].rearrange("(k p) s -> p k s", p=P), qkl).then_inc(lo_out.sem, 16)
                prev(st_ps, sp, b)
                hi_out.wait(sp, b)
                for part, at in ((0, 0), (0, 64), (1, 32)):
                    if part == 1:
                        lo_out.wait(sp, b)
                    sp.dma_start(qst[at:at + 32, :, :].bitcast(FP32), qk_d[part, 0:D].rearrange("(q r) s -> r q s", r=32)).then_inc(stack_in.sem, 16)
                    for e in range(2):
                        at_k = {(0, 0): 0, (0, 64): 32, (1, 32): 64}[(part, at)] + DH * e
                        sp.dma_start(kst[at_k:at_k + DH, :, :].rearrange("r (q e) s -> r q e s", e=2)[:, :, e, :].bitcast(FP32),
                                     qk_d[part, D:2 * D].rearrange("(q e r) s -> r q e s", e=2, r=DH)[:, :, e, :]).then_inc(stack_in.sem, 16)

            def nrows(b):
                nrow_ok.wait(sp, b)
                for r in range(4):
                    sp.dma_start(qst[96 + r:97 + r, :, :].bitcast(FP32), nrow[r * PAIRS:(r + 1) * PAIRS, :].bitcast(FP32)).then_inc(nrow_in.sem, 16)

            def store(b):
                res_ok.wait(sp, b)
                sp.dma_start(out[b].rearrange("(c p) d -> p c d", p=P), res[:]).then_inc(res_out.sem, 16)

            steps = {"X.load": load, "Y.stack": stack, "Y.nrows": nrows, "Z.store": store}
            run(sp, steps, """
                X.load Y.stack Y.nrows Z.store""")
            sp.wait_ge(res_out.sem, 16 * B)

        @block.gpsimd
        def _(pool):
            pool.memset(ident[:], 0.0).then_inc(build_ok.sem, 1)
            pool.wait_ge(build_ok.sem, 1)
            pool.affine_select(out=ident[:], in_=ident[:], compare_op=ALU.not_equal, fill=1.0, base=0,
                               pattern=[[-1, P]], channel_multiplier=1).then_inc(ident_ok.sem, 1)
            pool.memset(sel[:], 0.0)
            pool.memset(mask8[:], 1.0)
            pool.memset(mask4[:], 1.0)
            pool.memset(mhalf[:], -0.5)
            pool.memset(nz4[:], 1.0)
            pool.memset(prob[:], 0.0)
            pool.memset(vv[:, :, :, DH:], 1.0).then_inc(build_ok.sem, 1)
            pool.wait_ge(build_ok.sem, 2)
            pool.affine_select(out=sel[:], in_=sel[:], compare_op=ALU.not_equal, fill=1.0, base=0,
                               pattern=[[-1, 2], [-2, 2], [-4, M]], channel_multiplier=1)
            pool.affine_select(out=mask8[:], in_=mask8[:], compare_op=ALU.is_ge, fill=0.0, base=0,
                               pattern=[[-DH, 8]], channel_multiplier=1)
            pool.affine_select(out=mask4[:], in_=mask4[:], compare_op=ALU.is_ge, fill=0.0, base=0,
                               pattern=[[-MP, 4]], channel_multiplier=1).then_inc(build_ok.sem, 1)
            pool.wait_ge(build_ok.sem, 3)
            pool.affine_select(out=mask8[:], in_=mask8[:], compare_op=ALU.is_ge, fill=0.0, base=DH - 1,
                               pattern=[[DH, 8]], channel_multiplier=-1)
            pool.affine_select(out=mask4[:], in_=mask4[:], compare_op=ALU.is_ge, fill=0.0, base=M - 1,
                               pattern=[[MP, 4]], channel_multiplier=-1).then_inc(consts_ok.sem, 1)
            pool.wait_ge(zero_ok.sem, 2)
            pool.wait_ge(consts_ok.sem, 1)
            ones = kst[96:100, :, :].rearrange("r (q e) s -> r q e s", e=2)
            pool.affine_select(out=ones, in_=ones.bitcast(FP32), compare_op=ALU.is_ge, fill=0.0, base=0,
                               pattern=[[0, PAIRS], [-2, 2], [0, S]], channel_multiplier=1).then_inc(build_ok.sem, 1)
            pool.wait_ge(build_ok.sem, 4)
            pool.affine_select(out=ones, in_=ones.bitcast(FP32), compare_op=ALU.is_ge, fill=0.0, base=1,
                               pattern=[[0, PAIRS], [2, 2], [0, S]], channel_multiplier=-1).then_inc(consts_ok.sem, 1)
            pool.wait_ge(consts_ok.sem, 2)

            def low(into, whole, high, signal):
                pool.tensor_tensor(into, whole, high.bitcast(FP32), ALU.subtract).then_inc(signal.sem, 1)

            def selfl(b):
                selfh_ok.wait(pool, b)
                low(splx[:, 1], self32[:], splx[:, 0], selfl_ok)

            def aadd(c):
                def step(b):
                    am_ok.wait(pool, b, c + 1)
                    msk_ok.wait(pool, b)
                    pool.tensor_tensor(aff[:, c], aff[:, c], off[:, :, c, :].unsqueeze(2).broadcast_to([P, 2, H, M]),
                                       ALU.add).then_inc(aa_ok.sem, 1)
                return step

            def asub(c):
                def step(b):
                    amx_ok.wait(pool, b, c + 1)
                    t = aff[:, c].rearrange("p d h m -> p (d h) m")
                    pool.tensor_tensor(t, t, amx[:, c, :].unsqueeze(2).broadcast_to([P, 2 * H, M]),
                                       ALU.subtract).then_inc(asub_ok.sem, 1)
                return step

            def aprob(c):
                def step(b):
                    arc_ok.wait(pool, b, c + 1)
                    if c == 0:
                        prev(pT_ps, pool, b)
                    else:
                        pT_ps.wait(pool, b, 2)
                    pool.tensor_tensor(prob[:, :, 0:M], aff[:, c].rearrange("p d h m -> p (d h) m"),
                                       arc[:, c, :].unsqueeze(2).broadcast_to([P, 2 * H, M]), ALU.mult).then_inc(prob_ok.sem, 1)
                return step

            def pow1(b):
                v1_ok.wait(pool, b)
                pool.tensor_tensor(r1[:], v1[:], mhalf[:], ALU.pow).then_inc(r1_ok.sem, 1)

            def nxl(b):
                nxh_ok.wait(pool, b)
                low(sply[:, 1], nx32, sply[:, 0], nxl_ok)

            def x1bias(b):
                x1_ok.wait(pool, b)
                prev(x2_ok, pool, b)
                pool.tensor_tensor(x1b[:], x1[:], bo[:].unsqueeze(1).broadcast_to([P, TC, D]), ALU.add).then_inc(x1b_ok.sem, 1)

            def radd(c):
                def step(b):
                    rot_ok.wait(pool, b, c + 1)
                    pool.tensor_tensor(t1[:, c], t1[:, c], t2[:, c], ALU.add).then_inc(radd_ok.sem, 1)
                return step

            def qklow(n):
                def step(b):
                    qkh_ok.wait(pool, b, n + 1)
                    pool.tensor_tensor(qkl[:, 2 * n:2 * n + 2].bitcast(F32R), qk32, qkh[:, 2 * n:2 * n + 2],
                                       ALU.subtract).then_inc(qkl_ok.sem, 1)
                return step

            def alow(b):
                ah_ok.wait(pool, b)
                low(spla[:, 1], a32, spla[:, 0], al_ok)

            def pow2(b):
                v2_ok.wait(pool, b)
                pool.tensor_tensor(r2[:], v2[:], mhalf[:], ALU.pow).then_inc(r2_ok.sem, 1)

            def nzl(b):
                nzh_ok.wait(pool, b)
                low(splz[:, 1], nz32, splz[:, 0], nzl_ok)

            def hlow(j):
                def step(b):
                    hh_ok.wait(pool, b, j + 1)
                    low(hs[:, j % 2, 1], g32[:, j % 2], hs[:, j % 2, 0], hl_ok)
                return step

            steps = {"X.selfl": selfl, "Y.pow": pow1, "Y.nxl": nxl, "Y.x1b": x1bias, "Y.alow": alow, "Z.pow": pow2, "Z.nzl": nzl}
            for c in range(TC):
                steps |= {f"X.aadd{c}": aadd(c), f"X.asub{c}": asub(c), f"X.aprob{c}": aprob(c), f"Y.radd{c}": radd(c), f"Y.qkl{c}": qklow(c)}
            for j in range(NJ):
                steps[f"Z.hl{j}"] = hlow(j)
            run(pool, steps, """
                Y.alow-1 Y.pow X.selfl Y.nxl Z.pow Y.radd0 Y.radd1 Z.nzl Y.qkl0 Y.qkl1 X.aadd0 Z.hl0 X.aadd1 X.asub0
                X.asub1 Z.hl1 Y.x1b X.aprob0 X.aprob1 Z.hl2 Z.hl3""")

        @block.scalar
        def _(act):
            ident_fn = ACT.Identity
            act.wait_ge(vec_in.sem, 7 * 16)
            act.wait_ge(c_ps.sem, 2)
            for n in range(2):
                for k in range(KC):
                    at = 2 * n + k
                    ins = act.activation(hT[:, n, k, :], ps[:, 1, at * B:(at + 1) * B], ACT.Silu, bias=vec[:, V_B1 + at:V_B1 + at + 1])
            ins.then_inc(h_ok.sem, 1)

            def xh(b):
                xT_ps.wait(act, b)
                prev(q0_ps, act, b)
                act.activation(splx[:, 0], ps[:, BANK["xT"]].rearrange("p (k s) -> p k s", k=KC), ACT.Copy).then_inc(xh_ok.sem, 1)

            def nzt(b):
                nzT_ps.wait(act, b)
                prev(self_ps, act, b)
                act.activation(nzT[:], ps[0:4, BANK["nzT"], 0:S], ACT.Copy).then_inc(nzT_ok.sem, 1)

            def selfc(b):
                self_ps.wait(act, b)
                prev(y_ok, act, b)
                act.activation(self32[:], ps[:, BANK["self"]].rearrange("p (k s) -> p k s", k=KC), ACT.Copy).then_inc(self_ok.sem, 1)

            def kvrep(b):
                self_ok.wait(act, b)
                prev(v0_ps, act, b)
                act.activation(kvr[:], self32[:, :, 0:MP].unsqueeze(2).broadcast_to([P, KC, 4, MP]), ACT.Copy).then_inc(kvr_ok.sem, 1)

            def q0c(d):
                def step(b):
                    q0_ps.wait(act, b, d + 1)
                    for k in range(KC):
                        at = V_BQ0 + 2 * d + k
                        ins = act.activation(q0T[:, d, k, :], ps[:, BANK[f"q0.{d}"], k * S:(k + 1) * S], ident_fn, bias=vec[:, at:at + 1])
                    ins.then_inc(q0T_ok.sem, 1)
                return step

            def aexp(c):
                def step(b):
                    asub_ok.wait(act, b, c + 1)
                    act.activation(aff[:, c], aff[:, c], ACT.Exp).then_inc(aexp_ok.sem, 1)
                return step

            def pTc(n):
                def step(b):
                    c, d = divmod(n, 2)
                    pT_ps.wait(act, b, n + 1)
                    act.activation(pT[:, d, :, c * P:(c + 1) * P], ps[:, BANK[f"pT.{n}"]].rearrange("p (g s) -> p g s", g=4),
                                   ACT.Copy).then_inc(pT_ok.sem, 1)
                return step

            def square1(b):
                x1_ok.wait(act, b)
                prev(al_ok, act, b)
                for c in range(TC):
                    ins = act.activation(xr[:, c], x1[:, c], ACT.Square, accum_out=ss1[:, c:c + 1])
                    ins.then_inc(ss1_ok.sem, 1)

            def nxc(b):
                nx_ps.wait(act, b)
                cur1_ok.wait(act, b)
                for k in range(KC):
                    ins = act.activation(nx32[:, k, :], ps[:, BANK["nx"], k * S:(k + 1) * S], ident_fn,
                                         scale=cur1[:, k:k + 1], bias=cur1[:, 2 + k:3 + k])
                ins.then_inc(nx_ok.sem, 1)

            def vcopy(b):
                v_ps.wait(act, b)
                prev(pv_ps, act, b)
                act.activation(vv[:, :, :, 0:DH], ps[:, BANK["v"]].rearrange("p (c h d) -> p c h d", c=TC, h=H), ACT.Copy).then_inc(vv_ok.sem, 1)

            def nrowc(b):
                nmT_ps.wait(act, b)
                prev(nrow_in, act, b)
                act.activation(nrow[:], ps[0:4 * PAIRS, BANK["nmT"], 0:S], ACT.Copy).then_inc(nrow_ok.sem, 1)

            def exph(h):
                def step(b):
                    st_ps.wait(act, b, h + 1)
                    if h == 0:
                        hi_out.wait(act, b)
                        lo_out.wait(act, b)
                    if h >= 8:
                        pv_ps.wait(act, b, (h - 8) // 4 + 1)
                    act.activation(ex[:, h % 8], ps[:, h % 2].rearrange("p (c s) -> p c s", c=TC), ACT.Exp, scale=SCALE).then_inc(ex_ok.sem, 1)
                return step

            def oc(n):
                def step(b):
                    pv_ps.wait(act, b, 2 * n + 2)
                    act.activation(oT32[:, 2 * n:2 * n + 2, :], ps[:, 2].rearrange("p (g s) -> p g s", g=2), ACT.Copy).then_inc(o_ok.sem, 1)
                return step

            def square2(b):
                x2_ok.wait(act, b)
                prev(res_out, act, b)
                for c in range(TC):
                    act.activation(xr2[:, c], x2[:, c], ACT.Square, accum_out=ss2[:, c:c + 1]).then_inc(ss2_ok.sem, 1)

            def nzc(b):
                nz_ps.wait(act, b)
                cur2_ok.wait(act, b)
                prev(hl_ok, act, b)
                for k in range(KC):
                    ins = act.activation(nz32[:, k, :], ps[:, BANK["nz"], k * S:(k + 1) * S], ident_fn,
                                         scale=cur2[:, k:k + 1], bias=cur2[:, 2 + k:3 + k])
                ins.then_inc(nz_sb.sem, 1)

            def gelu(j):
                def step(b):
                    g_ps.wait(act, b, j + 1)
                    if j >= 2:
                        hl_ok.wait(act, b, j - 1)
                    else:
                        prev(hl_ok, act, b, NJ - 1 + j)
                    act.activation(g32[:, j % 2], ps[:, BANK[f"g.{j}"]].rearrange("p (k s) -> p k s", k=2), ACT.Gelu).then_inc(gelu_ok.sem, 1)
                return step

            steps = {"X.xh": xh, "X.nzt": nzt, "X.self": selfc, "X.kvr": kvrep, "Y.sq": square1, "Y.nx": nxc, "Y.v": vcopy,
                     "Y.nrow": nrowc, "Z.sq": square2, "Z.nz": nzc}
            for n in range(2):
                steps |= {f"X.q0{n}": q0c(n), f"X.aexp{n}": aexp(n), f"Y.o{n}": oc(n)}
            for n in range(4):
                steps |= {f"X.pT{n}": pTc(n), f"Z.gelu{n}": gelu(n)}
            for h in range(H):
                steps[f"Y.exp{h}"] = exph(h)
            run(act, steps, """
                Y.exp0-1 Y.exp1-1 Y.exp2-1 Y.exp3-1 Y.exp4-1 Y.exp5-1 Y.exp6-1 Y.exp7-1 Y.exp8-1 Y.exp9-1 Y.exp10-1
                Y.exp11-1 Y.exp12-1 Y.exp13-1 Y.o0-1 Y.exp14-1 Y.exp15-1 Y.o1-1 X.xh X.nzt Y.sq X.self Y.nx X.kvr Z.sq
                X.q00 Z.nz X.q01 Z.gelu0 Z.gelu1 X.aexp0 X.aexp1 X.pT0 Y.v X.pT1 Z.gelu2 X.pT2 X.pT3 Z.gelu3 Y.nrow""")

        @block.vector
        def _(dve):
            def high(into, whole, signal):
                dve.tensor_copy(into, whole).then_inc(signal.sem, 1)

            dve.memset(kst[:].bitcast(FP32), 0.0).then_inc(zero_ok.sem, 1)
            dve.wait_ge(zero_ok.sem, 1)
            dve.memset(kst[96:100, :, :].bitcast(FP32), 1.0).then_inc(zero_ok.sem, 1)

            dve.wait_ge(vec_in.sem, 7 * 16)
            dve.tensor_copy(qrow[:, 2, :], b32)
            dve.wait_ge(c_ps.sem, 1)
            dve.tensor_copy(q32, ps[0:B, 0, 0:D]).then_inc(c_sb.sem, 1)
            dve.wait_ge(c_sb.sem, 1)
            dve.tensor_copy(qrow[:, 0, :], q32).then_inc(c_sb.sem, 1)
            dve.wait_ge(c_sb.sem, 2)
            dve.tensor_tensor(qrow[:, 1, :], q32, qrow[:, 0, :].bitcast(FP32), ALU.subtract)
            dve.tensor_tensor(qrow[:, 3, :], b32, qrow[:, 2, :].bitcast(FP32), ALU.subtract).then_inc(qrow_ok.sem, 1)

            dve.tensor_tensor(vec[:, V_BOUT:V_BOUT + 2], vec[:, V_BOUT:V_BOUT + 2], vec[:, V_BOUT + 2:V_BOUT + 4], ALU.add).then_inc(bout_ok.sem, 1)
            for n, k in enumerate((3, 2)):
                dve.tensor_scalar(rbT[:, k, :], rbT[:, 0, :], vec[:, V_BQK + k:V_BQK + k + 1], None, ALU.mult).then_inc(rb_ok.sem, 1)
                dve.wait_ge(rb_ok.sem, 2 * n + 1)
                dve.scalar_tensor_tensor(out=rbT[:, k, :], in0=rbT[:, 1, :], scalar=vec[:, V_BQKS + k:V_BQKS + k + 1],
                                         in1=rbT[:, k, :], op0=ALU.mult, op1=ALU.add).then_inc(rb_ok.sem, 1)
            tmp = x2[:]
            for k in range(2):
                dve.tensor_scalar(tmp[:, k, :], rbT[:, 0, :], vec[:, V_BQK + k:V_BQK + k + 1], None, ALU.mult).then_inc(rb_ok.sem, 1)
            dve.wait_ge(rb_ok.sem, 6)
            for k in range(2):
                dve.scalar_tensor_tensor(out=tmp[:, k, :], in0=rbT[:, 1, :], scalar=vec[:, V_BQKS + k:V_BQKS + k + 1],
                                         in1=tmp[:, k, :], op0=ALU.mult, op1=ALU.add).then_inc(rb_ok.sem, 1)
            dve.wait_ge(rb_ok.sem, 8)
            dve.tensor_copy(rbT[:, 0:2, :], tmp).then_inc(rb_ok.sem, 1)
            dve.wait_ge(rb_ok.sem, 9)

            for n, (a, z) in enumerate(staged):
                dve.wait_ge(stage_in[n % 2].sem, 16 * (n // 2 + 1))
                dve.tensor_copy(wh[:, a:z], stage[:, n % 2, 0:z - a]).then_inc(wsplit.sem, 1)
                dve.wait_ge(wsplit.sem, 2 * n + 1)
                dve.tensor_tensor(wl[:, a:z], stage[:, n % 2, 0:z - a], wh[:, a:z].bitcast(FP32), ALU.subtract).then_inc(wsplit.sem, 1)
                dve.wait_ge(wsplit.sem, 2 * n + 2)

            dve.wait_ge(c_ps.sem, 3)
            cc = ps[:, 1, 64:64 + 8 * B].rearrange("p (n a k b) -> p n a k b", n=2, a=2, k=KC)
            for n in range(2):
                for k in range(KC):
                    at = V_B2 + 4 * n + k
                    dve.tensor_scalar(tab[:, n, :, 2 + k], cc[:, n, 1, k, :], vec[:, at + 2:at + 3], None, ALU.add)
                    dve.tensor_scalar(tab[:, n, :, k], cc[:, n, 0, k, :], vec[:, at:at + 1], 1.0, ALU.add, ALU.add).then_inc(tab_ok.sem, 1)
                    dve.wait_ge(tab_ok.sem, 2 * (2 * n + k) + 1)
                    dve.tensor_scalar(tab[:, n, :, k], tab[:, n, :, k], vec[:, V_WN + 2 * n + k:V_WN + 2 * n + k + 1], None,
                                      ALU.mult).then_inc(tab_ok.sem, 1)
            dve.wait_ge(tab_ok.sem, 8)
            dve.wait_ge(consts_ok.sem, 1)

            def adjm(b):
                adj_in.wait(dve, b)
                prev(prob_ok, dve, b)
                r = adjR[:].rearrange("p (n l) -> p n l", l=L)
                c = adjC[:].rearrange("p (n l) -> p n l", l=L)
                pr, pc = prodR.rearrange("p (n l) -> p n l", l=L), prodC.rearrange("p (n l) -> p n l", l=L)
                flat = cw[:].rearrange("p a d c m -> p a d (c m)")
                dve.tensor_tensor(pc, c, wb[0:AQ * M, 0:L].unsqueeze(1).broadcast_to([AQ * M, AN, L]), ALU.mult)
                dve.tensor_tensor(pr, r, wb[:, 0:L].unsqueeze(1).broadcast_to([P, TC * M, L]), ALU.mult).then_inc(prod_ok.sem, 1)
                prev(adjT_ps, dve, b)
                dve.tensor_reduce(cwC[:, 0, :], c, AX.X, ALU.add)
                dve.tensor_reduce(flat[:, 0, 0, :], r, AX.X, ALU.add)
                prod_ok.wait(dve, b)
                dve.tensor_reduce(cwC[:, 1, :], pc, AX.X, ALU.add)
                dve.tensor_reduce(flat[:, 1, 0, :], pr, AX.X, ALU.add).then_inc(adj_ok.sem, 1)

            def mask(b):
                adjT_ps.wait(dve, b)
                dve.tensor_copy(cw[:, :, 1].rearrange("p a c m -> p a (c m)"),
                                ps[:, BANK["adjT"], 0:4 * M].rearrange("p (a n) -> p a n", a=2)).then_inc(cw_ok.sem, 1)
                cw_ok.wait(dve, b)
                adj_ok.wait(dve, b)
                prev(aa_ok, dve, b)
                cnt, ws = (cw[:, a].rearrange("p d c m -> p (d c m)") for a in range(2))
                mf, of = msk[:].rearrange("p d c m -> p (d c m)"), off[:].rearrange("p d c m -> p (d c m)")
                dve.tensor_scalar(mf, cnt, 0.0, SCALE, ALU.is_gt, ALU.mult)
                dve.tensor_scalar(of, cnt, 0.0, NEG, ALU.is_le, ALU.mult).then_inc(off_ok.sem, 1)
                off_ok.wait(dve, b)
                dve.scalar_tensor_tensor(out=of, in0=ws, scalar=wb[:, L:L + 1], in1=of, op0=ALU.add, op1=ALU.add).then_inc(msk_ok.sem, 1)

            def nz(b):
                x_in.wait(dve, b)
                dve.tensor_reduce(rs[:], x_tok[:], AX.X, ALU.add).then_inc(rs_ok.sem, 1)
                rs_ok.wait(dve, b)
                prev(nzT_ps, dve, b)
                dve.tensor_scalar(nz4[:, :, 0:2], rs[:].unsqueeze(2).broadcast_to([P, TC, 2]), 0.0, None, ALU.not_equal).then_inc(nz_ok.sem, 1)

            def xl(b):
                xh_ok.wait(dve, b)
                dve.tensor_tensor(splx[:, 1], ps[:, BANK["xT"]].rearrange("p (k s) -> p k s", k=KC), splx[:, 0].bitcast(FP32),
                                  ALU.subtract).then_inc(xl_ok.sem, 1)

            def selfh(b):
                self_ok.wait(dve, b)
                high(splx[:, 0], self32[:], selfh_ok)

            def kb(b):
                k0_ps.wait(dve, b)
                for d in range(2):
                    for k in range(KC):
                        at = V_BK0 + 2 * d + k
                        src = ps[:, BANK["k0"], (2 * d + k) * P:(2 * d + k) * P + M]
                        ins = dve.scalar_tensor_tensor(
                            out=kblk[:, d, k], in0=src.unsqueeze(1).broadcast_to([P, 8, M]), scalar=vec[:, at:at + 1],
                            in1=mask8[:].unsqueeze(2).broadcast_to([P, 8, M]), op0=ALU.add, op1=ALU.mult)
                ins.then_inc(kblk_ok.sem, 1)

            def am(c):
                def step(b):
                    aff_ps.wait(dve, b, c + 1)
                    msk_ok.wait(dve, b)
                    dve.tensor_tensor(aff[:, c], ps[:, 3:5, 0:H * M].rearrange("p d (h m) -> p d h m", h=H),
                                      msk[:, :, c, :].unsqueeze(2).broadcast_to([P, 2, H, M]), ALU.mult).then_inc(am_ok.sem, 1)
                return step

            def amax(c):
                def step(b):
                    aa_ok.wait(dve, b, c + 1)
                    dve.tensor_reduce(amx[:, c, :], aff[:, c].rearrange("p d h m -> p (d h) m"), AX.X, ALU.max).then_inc(amx_ok.sem, 1)
                return step

            def asums(c):
                def step(b):
                    aexp_ok.wait(dve, b, c + 1)
                    dve.tensor_reduce(asum[:, c, :], aff[:, c].rearrange("p d h m -> p (d h) m"), AX.X, ALU.add).then_inc(asum_ok.sem, 1)
                    asum_ok.wait(dve, b, c + 1)
                    dve.reciprocal(arc[:, c, :], asum[:, c, :]).then_inc(arc_ok.sem, 1)
                return step

            def vb(b):
                v0_ps.wait(dve, b)
                prev(y_ps, dve, b)
                dve.tensor_tensor(vblk[:].rearrange("p d g (h n) -> p (d g) h n", h=4),
                                  ps[:, BANK["v0"]].rearrange("p (g h n) -> p g h n", h=4, n=DH),
                                  mask4[:].unsqueeze(1).unsqueeze(3).broadcast_to([P, 8, 4, DH]), ALU.mult).then_inc(vblk_ok.sem, 1)

            def yadd(b):
                y_ps.wait(dve, b)
                dve.tensor_tensor(yT, ps[:, BANK["y"]].rearrange("p (k s) -> p k s", k=KC), self32[:], ALU.add).then_inc(y_ok.sem, 1)
                y_ok.wait(dve, b)
                for k in range(KC):
                    ins = dve.tensor_scalar(yT[:, k, :], yT[:, k, :], vec[:, V_BOUT + k:V_BOUT + k + 1], 0.0, ALU.add, ALU.max)
                ins.then_inc(yr_ok.sem, 1)

            def x1add(b):
                x1_ps.wait(dve, b)
                prev(xr_ok, dve, b)
                prev(x1b_ok, dve, b)
                dve.tensor_tensor(x1[:], ps[:, BANK["x1"]].rearrange("p (c d) -> p c d", c=TC), x_tok[:], ALU.add).then_inc(x1_ok.sem, 1)

            def norm_in(ss, v, ss_ok, v_ok):
                def step(b):
                    ss_ok.wait(dve, b)
                    dve.tensor_scalar(v[:], ss[:], 1.0 / D, EPS, ALU.mult, ALU.add).then_inc(v_ok.sem, 1)
                return step

            def cur(n, now, ok, used):
                def step(b):
                    prev(used, dve, b)
                    dve.tensor_copy(now[:], tab[:, n, bass.ds(b, 1), :].rearrange("p b n -> p (b n)")).then_inc(ok.sem, 1)
                return step

            def scaled(src, dst, r, r_ok, ok):
                def step(b):
                    r_ok.wait(dve, b)
                    for c in range(TC):
                        ins = dve.tensor_scalar(dst[:, c], src[:, c], r[:, c:c + 1], None, ALU.mult)
                    ins.then_inc(ok.sem, 1)
                return step

            def nxh(b):
                nx_ok.wait(dve, b)
                prev(v_ps, dve, b)
                high(sply[:, 0], nx32, nxh_ok)

            def rot(c):
                def step(b):
                    qk_ps.wait(dve, b, c + 1)
                    src = ps[:, BANK[f"qk.{c}"]].rearrange("p (h a d) -> p h a d", a=2, d=DH // 2)
                    cs, sn = (rope[:, i, c, :].rearrange("p (a d) -> p a d", a=2).unsqueeze(1).broadcast_to([P, 2 * H, 2, DH // 2]) for i in range(2))
                    dve.tensor_tensor(t1[:, c].rearrange("p (h a d) -> p h a d", a=2, d=DH // 2), src, cs, ALU.mult)
                    dve.tensor_tensor(t2[:, c].rearrange("p (h a d) -> p h a d", a=2, d=DH // 2), src[:, :, ::-1, :], sn, ALU.mult).then_inc(rot_ok.sem, 1)
                return step

            def qkadd(n):
                def step(b):
                    qkT_ps.wait(dve, b, n + 1)
                    if n:
                        qkl_ok.wait(dve, b, n)
                    dve.tensor_tensor(qk32, ps[:, BANK[f"qkT.{n}"]].rearrange("p (k s) -> p k s", k=KC), rbT[:, 2 * n:2 * n + 2, :],
                                      ALU.add).then_inc(qk_ok.sem, 1)
                    qk_ok.wait(dve, b, n + 1)
                    dve.tensor_copy(qkh[:, 2 * n:2 * n + 2].bitcast(F32R), qk32).then_inc(qkh_ok.sem, 1)
                return step

            def mx(h):
                def step(b):
                    s_ps.wait(dve, b, h + 1)
                    if h == 0:
                        prev(nm4_ok, dve, b)
                    dve.tensor_reduce(nm[:, :, h], ps[:, h % 2].rearrange("p (c s) -> p c s", c=TC), AX.X, ALU.max, negate=True).then_inc(mx_ok.sem, 1)
                return step

            def nmx(b):
                mx_ok.wait(dve, b)
                prev(nmT_ps, dve, b)
                src = nm[:].rearrange("p c (q e) -> p c e q", e=2)
                for c in range(TC):
                    ins = dve.tensor_copy(nm4[:, c, :, 0, :], src[:, c])
                ins.then_inc(nmh_ok.sem, 1)
                nmh_ok.wait(dve, b)
                for c in range(TC):
                    ins = dve.tensor_tensor(nm4[:, c, :, 1, :], src[:, c], nm4[:, c, :, 0, :].bitcast(FP32), ALU.subtract)
                ins.then_inc(nm4_ok.sem, 1)

            def onorm(c):
                def step(b):
                    oT_ps.wait(dve, b, c + 1)
                    src = ps[:, BANK[f"oT.{c}"]].rearrange("p (h n) -> p h n", h=H)
                    dve.reciprocal(orc[:, c, :], src[:, :, DH]).then_inc(orc_ok.sem, 1)
                    orc_ok.wait(dve, b, c + 1)
                    dve.tensor_tensor(attn[:, c].rearrange("p (h n) -> p h n", h=H), src[:, :, 0:DH],
                                      orc[:, c, :].unsqueeze(2).broadcast_to([P, H, DH]), ALU.mult).then_inc(at_ok.sem, 1)
                return step

            def aadd32(b):
                aT_ps.wait(dve, b)
                dve.tensor_tensor(a32, ps[:, BANK["aT"]].rearrange("p (k s) -> p k s", k=KC),
                                  vec[:, V_BV:V_BV + 2].unsqueeze(2).broadcast_to([P, KC, S]), ALU.add).then_inc(a_ok.sem, 1)
                a_ok.wait(dve, b)
                prev(u_ps, dve, b)
                high(spla[:, 0], a32, ah_ok)

            def x2add(b):
                wo_ps.wait(dve, b)
                x1b_ok.wait(dve, b)
                dve.tensor_tensor(x2[:], ps[:, BANK["wo"]].rearrange("p (c d) -> p c d", c=TC), x1b[:], ALU.add).then_inc(x2_ok.sem, 1)

            def nzh(b):
                nz_sb.wait(dve, b)
                high(splz[:, 0], nz32, nzh_ok)

            def hmul(j):
                def step(b):
                    gelu_ok.wait(dve, b, j + 1)
                    u_ps.wait(dve, b, j + 1)
                    g = g32[:, j % 2]
                    dve.tensor_tensor(g, ps[:, BANK[f"u.{j}"]].rearrange("p (k s) -> p k s", k=2), g, ALU.mult).then_inc(hm_ok.sem, 1)
                    hm_ok.wait(dve, b, j + 1)
                    if j >= 2:
                        d_ps.wait(dve, b, j - 1)
                    else:
                        prev(d_ps, dve, b, NJ - 1 + j)
                    high(hs[:, j % 2, 0], g, hh_ok)
                return step

            def result(b):
                d_ps.wait(dve, b)
                dve.tensor_tensor(res[:], ps[:, BANK["d"]].rearrange("p (c d) -> p c d", c=TC), x2[:], ALU.add).then_inc(res_ok.sem, 1)

            steps = {"X.adjm": adjm, "X.mask": mask, "X.nz": nz, "X.xl": xl, "X.selfh": selfh, "X.kb": kb, "X.vb": vb,
                     "X.y": yadd, "X.x1": x1add, "Y.v": norm_in(ss1, v1, ss1_ok, v1_ok), "Y.cur": cur(0, cur1, cur1_ok, nx_ok),
                     "Y.xr": scaled(x1, xr, r1, r1_ok, xr_ok), "Y.nxh": nxh, "Y.nmx": nmx, "Y.a": aadd32,
                     "Z.x2": x2add, "Z.v": norm_in(ss2, v2, ss2_ok, v2_ok), "Z.cur": cur(1, cur2, cur2_ok, nz_sb),
                     "Z.xr": scaled(x2, xr2, r2, r2_ok, xr2_ok), "Z.nzh": nzh, "Z.res": result}
            for n in range(2):
                steps |= {f"X.am{n}": am(n), f"X.amax{n}": amax(n), f"X.asum{n}": asums(n), f"Y.rot{n}": rot(n),
                          f"Y.qk{n}": qkadd(n), f"Y.on{n}": onorm(n)}
            for h in range(H):
                steps[f"Y.mx{h}"] = mx(h)
            for j in range(NJ):
                steps[f"Z.h{j}"] = hmul(j)
            run(dve, steps, """
                X.x1-1 X.adjm X.nz Y.on0-1 Y.on1-1 X.xl Y.a-1 Y.v X.selfh Y.xr Y.nxh Z.x2 Z.v X.mask Z.xr Y.rot0 Y.rot1
                Z.nzh Y.qk0 X.kb Y.qk1 X.am0 Z.h0 Z.cur+1 X.am1 X.amax0 Z.h1 X.amax1 X.asum0 X.vb X.asum1 Y.mx0 Y.mx1
                Y.mx2 Y.mx3 Y.mx4 Y.mx5 Y.mx6 Y.mx7 Y.mx8 Y.mx9 Y.cur+1 Z.h2 Y.mx10 Y.mx11 Y.mx12 Y.mx13 Y.mx14 Y.mx15
                Y.nmx Z.h3 X.y Z.res""")

        @block.tensor
        def _(pe):
            def product(dst, lhs, rhs, ks, first_=True, last_=True, **kw):
                for n, k in enumerate(ks):
                    for m, (a, c) in enumerate(((0, 0), (0, 1), (1, 0))):
                        ins = pe.matmul(dst, lhs(a, k), rhs(c, k), start=first_ and n == 0 and m == 0,
                                        stop=last_ and n == len(ks) - 1 and m == 2, **kw)
                return ins

            def w(part, base, k, width, a, z):
                t = (wh, wl)[part]
                return t[:, base + k * width + a:base + k * width + z]

            pe.wait_ge(vec_in.sem, 7 * 16)
            pe.wait_ge(wc_in.sem, 16)
            for k in range(KC):
                ins = pe.matmul(ps[0:B, 0, 0:D], cT[:, k, :], wc[:, C_Q + k * D:C_Q + (k + 1) * D], start=k == 0, stop=k == KC - 1)
            ins.then_inc(c_ps.sem, 1)
            pe.wait_ge(wc2_in.sem, 16)
            for n in range(2):
                for o in range(KC):
                    for k in range(KC):
                        at = C_W1 + (n * KC + k) * D + o * P
                        ins = pe.matmul(ps[:, 1, (2 * n + o) * B:(2 * n + o + 1) * B], wc[:, at:at + P], cT[:, k, :], start=k == 0, stop=k == KC - 1)
            ins.then_inc(c_ps.sem, 1)
            pe.wait_ge(h_ok.sem, 1)
            for n in range(2):
                for o in range(4):
                    for k in range(KC):
                        at = C_W2 + (n * KC + k) * 2 * D + o * P
                        ins = pe.matmul(ps[:, 1, 64 + (4 * n + o) * B:64 + (4 * n + o + 1) * B], wc[:, at:at + P], hT[:, n, k, :],
                                        start=k == 0, stop=k == KC - 1)
            ins.then_inc(c_ps.sem, 1)
            pe.wait_ge(ident_ok.sem, 1)
            pe.wait_ge(consts_ok.sem, 1)
            pe.wait_ge(wsm_in.sem, 16)

            def transposes(dst, src, signal):
                for i in range(2):
                    for j in range(2):
                        ins = pe.transpose(dst[:, i * S + j * P:i * S + (j + 1) * P], src(i, j), ident[:])
                ins.then_inc(signal.sem, 1)

            def xT(b):
                bk = bank_free(pe, X_USES, "xT", b)
                x_in.wait(pe, b)
                transposes(ps[:, bk], lambda k, c: x_tok[:, c, k * P:(k + 1) * P], xT_ps)

            def nzTt(b):
                bk = bank_free(pe, X_USES, "nzT", b)
                nz_ok.wait(pe, b)
                for c in range(TC):
                    ins = pe.transpose(ps[0:4, bk, c * P:(c + 1) * P], nz4[:, c, :], ident[:])
                ins.then_inc(nzT_ps.sem, 1)

            def selfm(b):
                bk = bank_free(pe, X_USES, "self", b)
                xl_ok.wait(pe, b)
                nzT_ok.wait(pe, b)
                q4_in.wait(pe, b)
                if first(b):
                    pe.wait_ge(wsplit.sem, 4)
                for o in range(KC):
                    dst = ps[:, bk, o * S:(o + 1) * S]
                    product(dst, lambda a, k: w(a, W_SELF, k, D, o * P, (o + 1) * P), lambda a, k: splx[:, a, k, :], range(KC), last_=False)
                    ins = pe.matmul(dst, q4[:, o * P:(o + 1) * P], nzT[:], start=False, stop=True)
                ins.then_inc(self_ps.sem, 1)

            def adjT(b):
                bk = bank_free(pe, X_USES, "adjT", b)
                adj_ok.wait(pe, b)
                for a in range(2):
                    for j in range(2):
                        ins = pe.matmul(ps[64 * j:64 * j + 64, bk, a * 2 * M:(a + 1) * 2 * M], cwC[:, a, :],
                                        sel[:, j].rearrange("p n m -> p (n m)"), start=True, stop=True)
                ins.then_inc(adjT_ps.sem, 1)

            def q0(d):
                def step(b):
                    bk = bank_free(pe, X_USES, f"q0.{d}", b)
                    selfl_ok.wait(pe, b)
                    for o in range(KC):
                        ins = product(ps[:, bk, o * S:(o + 1) * S], lambda a, k: w(a, W_Q0 + d * 2 * D, k, D, o * P, (o + 1) * P),
                                      lambda a, k: splx[:, a, k, :], range(KC))
                    ins.then_inc(q0_ps.sem, 1)
                return step

            def k0(b):
                bk = bank_free(pe, X_USES, "k0", b)
                self_ok.wait(pe, b)
                for d in range(2):
                    for o in range(KC):
                        at = (2 * d + o) * P
                        for k in range(KC):
                            ins = pe.matmul(ps[:, bk, at:at + P], wsm[:, 0, d, k, o * P:(o + 1) * P], self32[:, k, 0:P], start=k == 0, stop=k == KC - 1)
                ins.then_inc(k0_ps.sem, 1)

            def affm(c):
                def step(b):
                    bank_free(pe, X_USES, f"aff.{c}", b)
                    bank_free(pe, X_USES, f"aff.{c}'", b)
                    q0T_ok.wait(pe, b)
                    kblk_ok.wait(pe, b)
                    for d in range(2):
                        for k in range(KC):
                            ins = pe.matmul(ps[:, 3 + d, k * 8 * M:(k + 1) * 8 * M], q0T[:, d, k, c * P:(c + 1) * P],
                                            kblk[:, d, k].rearrange("p h m -> p (h m)"), start=True, stop=True)
                    ins.then_inc(aff_ps.sem, 1)
                return step

            def v0(b):
                bk = bank_free(pe, X_USES, "v0", b)
                kvr_ok.wait(pe, b)
                for d in range(2):
                    for k in range(KC):
                        ins = pe.matmul(ps[:, bk, d * D:(d + 1) * D], kvr[:, k].rearrange("p r m -> p (r m)"), wsm[:, 1, d, k, :],
                                        start=k == 0, stop=k == KC - 1)
                ins.then_inc(v0_ps.sem, 1)

            def pTt(n):
                def step(b):
                    c, d = divmod(n, 2)
                    bk = bank_free(pe, X_USES, f"pT.{n}", b)
                    prob_ok.wait(pe, b, c + 1)
                    for g in range(4):
                        at = d * H + 4 * g
                        ins = pe.transpose(ps[:, bk, g * P:(g + 1) * P], prob[:, at:at + 4, :].rearrange("p h m -> p (h m)"), ident[:])
                    ins.then_inc(pT_ps.sem, 1)
                return step

            def y(b):
                bk = bank_free(pe, X_USES, "y", b)
                pT_ok.wait(pe, b)
                vblk_ok.wait(pe, b)
                for o in range(KC):
                    for d in range(2):
                        for j in range(2):
                            ins = pe.matmul(ps[64 * j:64 * j + 64, bk, o * S:(o + 1) * S], vblk[:, d, 2 * o + j, :], pT[:, d, 2 * o + j, :],
                                            start=d == 0, stop=d == 1)
                ins.then_inc(y_ps.sem, 1)

            def x1T(b):
                bk = bank_free(pe, X_USES, "x1", b)
                yr_ok.wait(pe, b)
                transposes(ps[:, bk], lambda c, k: yT[:, k, c * P:(c + 1) * P], x1_ps)

            def nxT(b):
                bk = bank_free(pe, Y_USES, "nx", b)
                xr_ok.wait(pe, b)
                transposes(ps[:, bk], lambda k, c: xr[:, c, k * P:(k + 1) * P], nx_ps)

            def qk(c):
                def step(b):
                    bk = bank_free(pe, Y_USES, f"qk.{c}", b)
                    nxl_ok.wait(pe, b)
                    if first(b) and c == 0:
                        pe.wait_ge(wsplit.sem, 2 * NSTAGE)
                    product(ps[:, bk, :], lambda a, k: sply[:, a, k, c * P:(c + 1) * P], lambda a, k: w(a, W_QK, k, 2 * D, 0, 2 * D),
                            range(KC)).then_inc(qk_ps.sem, 1)
                return step

            def v(b):
                bk = bank_free(pe, Y_USES, "v", b)
                for c in range(TC):
                    ins = product(ps[:, bk, c * D:(c + 1) * D], lambda a, k: sply[:, a, k, c * P:(c + 1) * P],
                                  lambda a, k: w(a, W_V, k, D, 0, D), range(KC))
                ins.then_inc(v_ps.sem, 1)

            def qkT(n):
                def step(b):
                    bk = bank_free(pe, Y_USES, f"qkT.{n}", b)
                    radd_ok.wait(pe, b)
                    transposes(ps[:, bk], lambda k, c: t1[:, c, (2 * n + k) * P:(2 * n + k + 1) * P], qkT_ps)
                return step

            def s(h):
                def step(b):
                    bk = bank_free(pe, Y_USES, f"s.{h}", b)
                    if h == 0:
                        stack_in.wait(pe, b)
                        if first(b):
                            pe.wait_ge(consts_ok.sem, 2)
                    for c in range(TC):
                        ins = pe.matmul(ps[:, bk, c * S:(c + 1) * S], qst[0:96, h // 2, c * P:(c + 1) * P], kst[0:96, h, :], start=True, stop=True)
                    ins.then_inc(s_ps.sem, 1)
                return step

            def nmT(b):
                bk = bank_free(pe, Y_USES, "nmT", b)
                nm4_ok.wait(pe, b)
                for c in range(TC):
                    ins = pe.transpose(ps[0:4 * PAIRS, bk, c * P:(c + 1) * P],
                                       nm4[:, c].rearrange("p e a q -> p (e a q)").bitcast(FP32), ident[:])
                ins.then_inc(nmT_ps.sem, 1)

            def st(h):
                def step(b):
                    bk = bank_free(pe, Y_USES, f"st.{h}", b)
                    if h == 0:
                        nrow_in.wait(pe, b)
                    for c in range(TC):
                        ins = pe.matmul(ps[:, bk, c * S:(c + 1) * S], kst[0:100, h, c * P:(c + 1) * P], qst[0:100, h // 2, :], start=True, stop=True)
                    ins.then_inc(st_ps.sem, 1)
                return step

            def pv(g):
                def step(b):
                    if g % 2 == 0:
                        bank_free(pe, Y_USES, f"o.{g // 2}", b)
                    ex_ok.wait(pe, b, 4 * g + 4)
                    if g == 0:
                        vv_ok.wait(pe, b)
                    for c in range(TC):
                        for j in range(4):
                            h = 4 * g + j
                            ins = pe.matmul(ps[32 * j:32 * j + 32, 2, (g % 2) * S:(g % 2 + 1) * S], vv[:, c, h, :], ex[:, h % 8, c, :],
                                            start=c == 0, stop=c == TC - 1)
                    ins.then_inc(pv_ps.sem, 1)
                return step

            def oT(c):
                def step(b):
                    bk = bank_free(pe, Y_USES, f"oT.{c}", b)
                    o_ok.wait(pe, b)
                    for g in range(4):
                        ins = pe.transpose(ps[:, bk, g * P:(g + 1) * P], oT32[:, g, c * P:(c + 1) * P], ident[:])
                    ins.then_inc(oT_ps.sem, 1)
                return step

            def aT(b):
                bk = bank_free(pe, Y_USES, "aT", b)
                at_ok.wait(pe, b)
                transposes(ps[:, bk], lambda k, c: attn[:, c, k * P:(k + 1) * P], aT_ps)

            def wo(b):
                bk = bank_free(pe, Z_USES, "wo", b)
                al_ok.wait(pe, b)
                for c in range(TC):
                    ins = product(ps[:, bk, c * D:(c + 1) * D], lambda a, k: spla[:, a, k, c * P:(c + 1) * P],
                                  lambda a, k: w(a, W_O, k, D, 0, D), range(KC))
                ins.then_inc(wo_ps.sem, 1)

            def nzTr(b):
                bk = bank_free(pe, Z_USES, "nz", b)
                xr2_ok.wait(pe, b)
                transposes(ps[:, bk], lambda k, c: xr2[:, c, k * P:(k + 1) * P], nz_ps)

            def hidden(name, base, j, signal):
                def step(b):
                    bk = bank_free(pe, Z_USES, f"{name}.{j}", b)
                    nzl_ok.wait(pe, b)
                    for i in range(2):
                        n = 2 * j + i
                        ins = product(ps[:, bk, i * S:(i + 1) * S], lambda a, k: w(a, base, k, FF, n * P, (n + 1) * P),
                                      lambda a, k: splz[:, a, k, :], range(KC))
                    ins.then_inc(signal.sem, 1)
                return step

            def down(j):
                def step(b):
                    if j == 0:
                        bank_free(pe, Z_USES, "d", b)
                    hl_ok.wait(pe, b, j + 1)
                    for c in range(TC):
                        ins = product(ps[:, 7, c * D:(c + 1) * D], lambda a, i: hs[:, j % 2, a, i, c * P:(c + 1) * P],
                                      lambda a, i: w(a, W_D, 2 * j + i, D, 0, D), range(2), first_=j == 0 and c == 0, last_=j == NJ - 1,
                                      skip_group_check=True)
                    ins.then_inc(d_ps.sem, 1)
                return step

            steps = {"X.xT": xT, "X.nzT": nzTt, "X.self": selfm, "X.adjT": adjT, "X.k0": k0, "X.v0": v0, "X.y": y, "X.x1": x1T,
                     "Y.nx": nxT, "Y.v": v, "Y.nmT": nmT, "Y.aT": aT, "Z.wo": wo, "Z.nz": nzTr}
            for n in range(2):
                steps |= {f"X.q0{n}": q0(n), f"X.aff{n}": affm(n), f"Y.qk{n}": qk(n), f"Y.qkT{n}": qkT(n), f"Y.oT{n}": oT(n)}
            for n in range(4):
                steps |= {f"X.pT{n}": pTt(n), f"Y.pv{n}": pv(n), f"Z.g{n}": hidden("g", W_G, n, g_ps), f"Z.u{n}": hidden("u", W_U, n, u_ps),
                          f"Z.d{n}": down(n)}
            for h in range(H):
                steps |= {f"Y.s{h}": s(h), f"Y.st{h}": st(h)}
            run(pe, steps, """
                Y.st8-1 Y.st9-1 Y.pv1-1 Y.st10-1 Y.st11-1 X.xT Y.st12-1 Y.st13-1 Y.st14-1 Y.st15-1 Y.pv2-1 Y.pv3-1
                Y.oT0-1 Y.oT1-1 X.nzT Y.aT-1 X.self X.adjT Z.wo Y.nx X.q00 Y.qk0 Y.qk1 Z.nz X.q01 X.k0 Y.qkT0 Z.g0
                Y.qkT1 Z.u0 X.aff0 Z.g1 X.aff1 Z.u1 Y.v X.v0 Z.g2 Z.d0 Y.s0 Y.s1 Z.u2 Y.s2 Y.s3 Y.s4 Y.s5 X.pT0 Y.s6
                Y.s7 X.pT1 Y.s8 Y.s9 Z.d1 Y.s10 Y.s11 Z.g3 Y.s12 Y.s13 X.pT2 Y.s14 X.pT3 Y.s15 Z.u3 Y.nmT X.y Z.d2 Z.d3
                Y.st0 Y.st1 X.x1 Y.st2 Y.st3 Y.st4 Y.st5 Y.st6 Y.st7 Y.pv0""")


_IN = ["x", "adj", "condT", "wall", "wsmall", "wcond", "cols", "rows_in", "tabs"]


def kernel(**inputs):
    import numpy as np
    import concourse.bacc as bacc
    from concourse.bass_utils import run_bass_kernel_spmd

    f = {k: np.asarray(v) for k, v in inputs.items()}

    def rows(a):
        return a.reshape(-1, P, a.shape[1]).transpose(1, 0, 2).reshape(P, -1)

    def column(a):
        return a.reshape(-1, P).T

    def cat(parts):
        return np.ascontiguousarray(np.concatenate(parts, axis=1))

    w_self, wq0, wk0, wout = f["L0_cond_W_self"], f["L0_cond_Wq"], f["L0_cond_Wk"], f["L0_cond_Wout"]
    wqk = np.concatenate([f["L1_cond_wq"], f["L1_cond_wk"]], axis=1)
    bqk = np.concatenate([f["L1_cond_bq"], f["L1_cond_bk"]])
    bqk_swapped = bqk.reshape(-1, 2, DH // 2)[:, ::-1].reshape(-1)
    b2 = [f["L1_cond_t1_b2"], f["L1_cond_t2_b2"]]
    inv_freq = (np.float32(1.0) / np.float32(10000.0) ** (np.arange(0, DH, 2, dtype=np.float32) / np.float32(DH))).astype(np.float32)
    angle = np.arange(S, dtype=np.float32)[:, None] * np.concatenate([inv_freq, inv_freq])[None, :]
    sign = np.where(np.arange(DH) < DH // 2, -1.0, 1.0).astype(np.float32)
    cos, sin = np.cos(angle).astype(np.float32), (np.sin(angle) * sign).astype(np.float32)

    arrays = {
        "x": f["x"],
        "adj": f["mask_BxSxSx11_ik0"],
        "condT": np.ascontiguousarray(rows(f["cond_1024"].T)),
        "wall": cat([rows(w_self[:, :D].T), rows(wq0[0].T), rows(wq0[1].T), rows(wqk), rows(f["L1_cond_wv"]), rows(f["L1_cond_wo"]),
                     rows(f["L1_cond_w_gate"]), rows(f["L1_cond_w_up"]), rows(f["L1_cond_w_down"])]),
        "wsmall": cat([rows(wk0[0].T), rows(wk0[1].T), rows(wout[0].reshape(D, D).T), rows(wout[1].reshape(D, D).T)]),
        "wcond": cat([rows(w_self[:, D:].T), rows(f["L1_cond_t1_w1"]), rows(f["L1_cond_t2_w1"]), rows(f["L1_cond_t1_w2"]), rows(f["L1_cond_t2_w2"])]),
        "cols": cat([column(f["L0_cond_bq"].reshape(-1)), column(f["L0_cond_bk"].reshape(-1)), column(f["L0_cond_bout"].reshape(-1)),
                     column(f["L1_cond_bv"]), column(f["L1_cond_t1_b1"]), column(f["L1_cond_t2_b1"]), column(b2[0]), column(b2[1]),
                     column(f["L1_cond_w_norm1"]), column(f["L1_cond_w_norm2"]), column(bqk), column(bqk_swapped)]),
        "rows_in": cat([f["L1_cond_bo"][None], f["L0_cond_b_self"][None], f["L0_cond_w_bias"][None], f["L0_cond_b_bias"].reshape(1, 1)]),
        "tabs": cat([rows(cos), rows(sin), np.tile(cos.T, (P // DH, 1)), np.tile(sin.T, (P // DH, 1))]),
    }
    nc = bacc.Bacc("TRN2", target_bir_lowering=False, num_devices=1)
    args = [nc.dram_tensor(n, arrays[n].shape, mybir.dt.from_np(arrays[n].dtype), kind="ExternalInput").ap() for n in _IN]
    result = nc.dram_tensor("result", (B, S, D), FP32, kind="ExternalOutput").ap()
    build(nc, *args, result)
    r = run_bass_kernel_spmd(nc, [arrays], core_ids=[0])
    return r.results[0]["result"]
```

```python
import math
from contextlib import ExitStack

import concourse.bass as bass
import concourse.mybir as mybir

FP32 = mybir.dt.float32
F32R = mybir.dt.float32r
INT32 = mybir.dt.int32
ALU = mybir.AluOpType
ACT = mybir.ActivationFunctionType
AX = mybir.AxisListType

P = 128
B, S, D = 8, 256, 256
L = 11
M = 20
MP = 32
KN = 32
H, DH = 16, 16
FF = 1024
EPS = 1e-5
NEG = -9000000000000000.0
SCALE = 1.0 / math.sqrt(DH)
KC = D // P
TC = S // P
PAIRS = H // 2
EXR = 6
NFF = FF // P
NJ = NFF // 2
AQ = 4
AN = S // AQ

W_SELF, W_Q0, W_QK, W_V, W_O, W_G, W_U, W_D = 0, 512, 1536, 2560, 3072, 3584, 5632, 7680
W_ALL = 9728
PARTS = {"self": (W_SELF, 512), "q0": (W_Q0, 1024), "qk": (W_QK, 1024), "v": (W_V, 512), "o": (W_O, 512),
         "g": (W_G, 2048), "u": (W_U, 2048), "d": (W_D, 2048)}
PIECE = 512
PIECES = [(part, n) for part, (_, width) in PARTS.items() for n in range(width // PIECE)]
POOL_LOWS = ("o", "g", "d")
K_ID, K_SEL, K_M8, K_M4, K_ONES, K_ALL = 0, 128, 208, 216, 220, 236
V_BQ0, V_BK0, V_BOUT, V_BV, V_B1, V_B2, V_WN, V_BQK, V_BQKS, V_ALL = 0, 4, 8, 12, 14, 18, 26, 30, 34, 38
C_Q, C_W1, C_W2, C_ALL = 0, 512, 1536, 3584


class Signal:

    def __init__(self, sem, per):
        self.sem, self.per = sem, per

    def at(self, b, n=None):
        value = b * self.per + (self.per if n is None else n)
        assert not isinstance(value, int) or value > 0
        return value


def build(nc, x, adj, condT, wall, wsmall, wcond, cols, rows_in, tabs, consts_in, out):
    ctx = ExitStack()
    with ctx:
        def sb(name, shape, dt=FP32):
            return ctx.enter_context(nc.sbuf_tensor(name, shape, dt))

        def sig(name, per=1):
            return Signal(ctx.enter_context(nc.semaphore(name)), per)

        wh, wl = sb("wh", [P, W_ALL], F32R), sb("wl", [P, W_ALL], F32R)
        wsm = sb("wsm", [P, 2, 2, KC, D])
        kst = sb("kst", [P, H, S], F32R)
        qst = sb("qst", [P, PAIRS, S], F32R)
        rbT = sb("rbT", [P, 2 * KC, S])
        vec = sb("vec", [P, V_ALL])
        bo = sb("bo", [P, D])
        wb = sb("wb", [P, L + 1])
        rope = sb("rope", [P, 2, TC, DH])
        consts = sb("const_sb", [P, K_ALL])
        ident = consts[:, K_ID:K_ID + P]
        sel = consts[0:AQ * M, K_SEL:K_M8].rearrange("p (j a m) -> p j a m", j=2, a=2)
        mask8, mask4 = consts[:, K_M8:K_M4], consts[:, K_M4:K_ONES]
        mhalf = sb("mhalf", [P, TC])
        cT = sb("cT", [P, KC, B])
        hT = sb("hT", [P, 2, KC, B])
        tab = sb("tab", [P, 2, B, 4])
        cur1, cur2 = sb("cur1", [P, 4]), sb("cur2", [P, 4])
        x_tok = sb("x_tok", [P, TC, D])
        x_add = sb("x_add", [P, TC, D])
        adjR = sb("adjR", [P, TC * M * L], INT32)
        adjC = sb("adjC", [AQ * M, AN * L], INT32)
        cw = sb("cw", [P, 2, 2, TC, M])
        cwC = sb("cwC", [AQ * M, 2, AN])
        msk = sb("msk", [P, 2, TC, M])
        off = sb("off", [P, 2, TC, M])
        rs = sb("rs", [P, TC])
        nz4 = sb("nz4", [P, TC, 4])
        nzT = sb("nzT", [4, S], F32R)
        q4 = sb("q4", [4, D], F32R)
        splx = sb("splx", [P, 2, KC, S], F32R)
        self32 = sb("self32", [P, KC, S])
        kvr = sb("kvr", [P, KC, 4, MP])
        aff = sb("aff", [P, TC, 2, H, M])
        amx = sb("amx", [P, TC, 2 * H])
        asum = sb("asum", [P, TC, 2 * H])
        arc = sb("arc", [P, TC, 2 * H])
        prob = sb("prob", [P, 2 * H, MP])
        vblk = sb("vblk", [P, 2, 4, 64])
        l0 = sb("l0", [P, 2048])
        q0T = l0[:, 0:1024].rearrange("p (d k s) -> p d k s", d=2, k=KC)
        kblk = l0[:, 1024:1664].rearrange("p (d k h m) -> p d k h m", d=2, k=KC, h=8)
        pT = l0[:, :].rearrange("p (d g s) -> p d g s", d=2, g=4)
        yT = l0[:, 0:512].rearrange("p (k s) -> p k s", k=KC)
        prodC = aff[0:AQ * M].rearrange("p c d h m -> p (c d h m)")[:, 0:AN * L]
        prodR = aff[:].rearrange("p c d h m -> p (c d h m)")[:, AN * L:AN * L + TC * M * L]
        x1 = sb("x1", [P, TC, D])
        ss1, v1, r1 = sb("ss1", [P, TC]), sb("v1", [P, TC]), sb("r1", [P, TC])
        sply = sb("sply", [P, 2, KC, S], F32R)
        vv = sb("vv", [P, TC, H, 32])
        nm = sb("nm", [P, TC, H])
        nm4 = sb("nm4", [P, TC, 2, 2, PAIRS], F32R)
        nrow = sb("nrow", [4 * PAIRS, S], F32R)
        orc = sb("orc", [P, TC, H])
        xr = sb("xr", [P, TC, D])
        nx32 = xr[:].rearrange("p c d -> p (c d)").rearrange("p (k s) -> p k s", k=KC)
        ya = sb("ya", [P, 4608])
        t1 = ya[:, 0:1024].rearrange("p (c n) -> p c n", c=TC)
        t2 = ya[:, 1024:2048].rearrange("p (c n) -> p c n", c=TC)
        qk32 = ya[:, 2048:2560].rearrange("p (k s) -> p k s", k=KC)
        qkh = ya[:, 2560:3584].rearrange("p (k s) -> p k s", k=2 * KC)
        qkl = ya[:, 3584:4608].rearrange("p (k s) -> p k s", k=2 * KC)
        ex = ya[:, 0:EXR * 512].rearrange("p (h c s) -> p h c s", h=EXR, c=TC)
        oT32 = ya[:, 3072:4096].rearrange("p (g s) -> p g s", g=4)
        a32 = ya[:, 3072:3584].rearrange("p (k s) -> p k s", k=KC)
        attn = ya[:, 4096:4608].rearrange("p (c d) -> p c d", c=TC)
        wc = ya[:, 0:C_ALL]
        x1b, x2 = sb("x1b", [P, TC, D]), sb("x2", [P, TC, D])
        xr2 = sb("xr2", [P, TC, D])
        res = xr2
        ss2, v2, r2 = sb("ss2", [P, TC]), sb("v2", [P, TC]), sb("r2", [P, TC])
        splz = sb("splz", [P, 2, KC, S], F32R)
        spla = splz
        g32 = sb("g32", [P, 2, 2, S])
        nz32 = g32[:, 0]
        hs = sb("hs", [P, 2, 2, 2, S], F32R)
        qrow = hs[0:B, 0].rearrange("p a i s -> p (a i) s")
        q32, b32 = g32[0:B, 0, 0, :], g32[0:B, 0, 1, :]
        angles = g32[:, 1]

        slots = [ya[:, C_ALL + n * PIECE:C_ALL + (n + 1) * PIECE] for n in range(2)] + [
            t[:].rearrange("p c d -> p (c d)") for t in (x1b, x2, xr2, xr, x_add)]
        SLOTS_YA, SLOT_X1B, SLOT_X2, SLOT_XR2, SLOT_XR, SLOT_XA = (0, 1), 2, 3, 4, 5, 6
        last_piece = [[p for at, p in enumerate(PIECES) if at % len(slots) == slot][-1] for slot in range(len(slots))]

        q4_d = nc.dram_tensor("q4_d", [B, 4, D], FP32, kind="Internal").ap()
        qk_d = nc.dram_tensor("qk_d", [2, 2 * D, S], FP32, kind="Internal").ap()

        ps = ctx.enter_context(nc.psum_tensor("ps", [P, 8, 512], FP32))

        x_in, xa_in, adj_in, q4_in = sig("x_in", 16), sig("xa_in", 16), sig("adj_in", 32), sig("q4_in", 16)
        cond_in, brow_in, consts_arr, vec_in, wb_in, wc2_in, rope_in, angles_in, wsm_in, bo_in = (
            sig("cond_in", 32), sig("brow_in", 16), sig("consts_arr", 16), sig("vec_in", 16), sig("wb_in", 16), sig("wc2_in", 16),
            sig("rope_in", 16), sig("angles_in", 16), sig("wsm_in", 16), sig("bo_in", 16))
        w_in = [sig(f"w_in{n}", 16) for n in range(len(slots))]
        w_high = {p: sig(f"w_high_{p}", n // PIECE) for p, (_, n) in PARTS.items()}
        w_low = {p: sig(f"w_low_{p}", n // PIECE) for p, (_, n) in PARTS.items()}
        q4_out = sig("q4_out")
        hi_out, lo_out, stack_in, nrow_in, res_out = (
            sig("hi_out", 16), sig("lo_out", 16), sig("stack_in", 9 * 16), sig("nrow_in", 4 * 16), sig("res_out", 16))
        const_ok, zero_ok, ones_ok = sig("const_ok"), sig("zero_ok", 2), sig("ones_ok", 2)
        c_ps, c_sb, h_ok, rb_ok, tab_ok, qrow_ok, bout_ok = (
            sig("c_ps", 3), sig("c_sb", 2), sig("h_ok"), sig("rb_ok", 8), sig("tab_ok", 8), sig("qrow_ok"), sig("bout_ok"))
        xT_ps, nzT_ps, self_ps, adjT_ps, q0_ps, k0_ps, v0_ps = (
            sig("xT_ps"), sig("nzT_ps"), sig("self_ps", KC), sig("adjT_ps"), sig("q0_ps", 4), sig("k0_ps"), sig("v0_ps"))
        aff_ps, pT_ps, y_ps, x1_ps = sig("aff_ps", TC), sig("pT_ps", 2 * TC), sig("y_ps"), sig("x1_ps")
        nx_ps, qk_ps, v_ps, qkT_ps, s_ps, nmT_ps, st_ps, pv_ps, oT_ps, aT_ps = (
            sig("nx_ps"), sig("qk_ps", TC), sig("v_ps", TC), sig("qkT_ps", 2), sig("s_ps", H), sig("nmT_ps"), sig("st_ps", H),
            sig("pv_ps", 4), sig("oT_ps", TC), sig("aT_ps"))
        wo_ps, nz_ps, g_ps, u_ps, d_ps = sig("wo_ps", TC), sig("nz_ps"), sig("g_ps", 2 * NJ), sig("u_ps", 2 * NJ), sig("d_ps", TC * NJ)
        rs_ok, nz_ok, nzT_ok, xh_ok, xl_ok, self_ok, selfh_ok, selfl_ok, kvr_ok = (
            sig("rs_ok"), sig("nz_ok"), sig("nzT_ok"), sig("xh_ok"), sig("xl_ok"), sig("self_ok"), sig("selfh_ok"),
            sig("selfl_ok"), sig("kvr_ok"))
        prod_ok, adj_ok, cw_ok, off_ok, msk_ok = sig("prod_ok"), sig("adj_ok"), sig("cw_ok"), sig("off_ok"), sig("msk_ok")
        q0T_ok, kblk_ok, vblk_ok = sig("q0T_ok", 2), sig("kblk_ok"), sig("vblk_ok")
        am_ok, aa_ok, amx_ok, asub_ok, aexp_ok, asum_ok, arc_ok, prob_ok, pT_ok = (
            sig("am_ok", TC), sig("aa_ok", TC), sig("amx_ok", TC), sig("asub_ok", TC), sig("aexp_ok", TC),
            sig("asum_ok", TC), sig("arc_ok", TC), sig("prob_ok", TC), sig("pT_ok", 2 * TC))
        y_ok, yr_ok, x1_ok = sig("y_ok"), sig("yr_ok"), sig("x1_ok")
        cur1_ok, ss1_ok, v1_ok, r1_ok, xr_ok, nx_ok, nxh_ok, nxl_ok = (
            sig("cur1_ok"), sig("ss1_ok", TC), sig("v1_ok"), sig("r1_ok"), sig("xr_ok"), sig("nx_ok"), sig("nxh_ok"), sig("nxl_ok"))
        rot_ok, radd_ok, vv_ok, qk_ok, qkh_ok, qkl_ok = (
            sig("rot_ok", TC), sig("radd_ok", TC), sig("vv_ok"), sig("qk_ok", 2), sig("qkh_ok", 2), sig("qkl_ok", 2))
        mx_ok, nmh_ok, nm4_ok, nrow_ok, ex_ok, o_ok, orc_ok, at_ok, a_ok, ah_ok, al_ok = (
            sig("mx_ok", H), sig("nmh_ok"), sig("nm4_ok"), sig("nrow_ok"), sig("ex_ok", H), sig("o_ok", 2), sig("orc_ok", TC),
            sig("at_ok", TC), sig("a_ok"), sig("ah_ok"), sig("al_ok"))
        x1b_ok, x2_ok, cur2_ok, ss2_ok, v2_ok, r2_ok, xr2_ok, nz_sb, nzh_ok, nzl_ok = (
            sig("x1b_ok"), sig("x2_ok"), sig("cur2_ok"), sig("ss2_ok", TC), sig("v2_ok"), sig("r2_ok"), sig("xr2_ok"),
            sig("nz_sb"), sig("nzh_ok"), sig("nzl_ok"))
        gelu_ok, hm_ok, hh_ok, hl_ok, res_ok = sig("gelu_ok", NJ), sig("hm_ok", NJ), sig("hh_ok", NJ), sig("hl_ok", NJ), sig("res_ok")

        BANK = {"xT": 3, "nzT": 4, "self": 3, "adjT": 4, "q0": (3, 4), "k0": 3, "aff": 3, "v0": 3, "pT": (4, 3), "y": 4, "x1": 3,
                "nx": 2, "qk": (0, 1), "v": 2, "qkT": (0, 1), "nmT": 2, "o": 2, "oT": (0, 1), "aT": 2,
                "wo": 5, "nz": 6, "g": 5, "u": 6, "d": 7}

        def first(b):
            return isinstance(b, int) and b == 0

        block = ctx.enter_context(nc.Block())

        def step(f, b):
            if not isinstance(b, int) or 0 <= b < B:
                f(b)

        def once(f, b):
            if isinstance(b, int) and b == 0:
                f()

        def rounds(eng, round_, lead, lag):
            for it in range(-lead, 1 - lag):
                round_(it)
            with eng.Fori(1 - lag, B - lead) as it:
                round_(it)
            for it in range(B - lead, B - lag):
                round_(it)

        @block.sync
        def _(sp):
            def fetch(dst, src, signal):
                return lambda: sp.dma_start(dst, src).then_inc(signal.sem, 16)

            def cond():
                sp.dma_start(cT[:], condT.rearrange("p (k b) -> p k b", k=KC)).then_inc(cond_in.sem, 16)
                sp.dma_start(wc[:, 0:C_W1], wcond[:, 0:C_W1]).then_inc(cond_in.sem, 16)

            def weights(part, n):
                def step():
                    a, at = PARTS[part][0] + n * PIECE, PIECES.index((part, n))
                    if at >= len(slots):
                        before, m = PIECES[at - len(slots)]
                        sp.wait_ge(w_low[before].sem, w_low[before].at(0, m + 1))
                    sp.dma_start(slots[at % len(slots)], wall[:, a:a + PIECE]).then_inc(w_in[at % len(slots)].sem, 16)
                return step

            def qrows():
                sp.wait_ge(qrow_ok.sem, qrow_ok.at(0))
                sp.dma_start(q4_d.rearrange("b r n -> b (r n)"), qrow.rearrange("b r n -> b (r n)").bitcast(FP32)).then_inc(q4_out.sem, 16)

            def load_x(b):
                if not first(b):
                    sp.wait_ge(xT_ps.sem, xT_ps.at(b - 1))
                    sp.wait_ge(rs_ok.sem, rs_ok.at(b - 1))
                sp.dma_start(x_tok[:], x[b].rearrange("(c p) d -> p c d", p=P)).then_inc(x_in.sem, 16)

            def load_x_add(b):
                if not first(b):
                    sp.wait_ge(x1_ok.sem, x1_ok.at(b - 1))
                else:
                    part, n = last_piece[SLOT_XA]
                    sp.wait_ge(w_low[part].sem, w_low[part].at(0, n + 1))
                sp.dma_start(x_add[:], x[b].rearrange("(c p) d -> p c d", p=P)).then_inc(xa_in.sem, 16)

            def load_adj(b):
                if not first(b):
                    sp.wait_ge(adj_ok.sem, adj_ok.at(b - 1))
                sp.dma_start(adjR[:].rearrange("p (c n) -> p c n", c=TC),
                             adj[b, :, 0:M, :].rearrange("(c p) m l -> p c (m l)", p=P)).then_inc(adj_in.sem, 16)
                sp.dma_start(adjC[:], adj[b, 0:M].rearrange("m (q n) l -> (m q) (n l)", q=AQ)).then_inc(adj_in.sem, 16)

            def load_q(b):
                if first(b):
                    sp.wait_ge(q4_out.sem, 16)
                else:
                    sp.wait_ge(self_ps.sem, self_ps.at(b - 1))
                sp.dma_start(q4[:].bitcast(FP32), q4_d[b]).then_inc(q4_in.sem, 16)

            def stack(b):
                if not first(b):
                    sp.wait_ge(stack_in.sem, stack_in.at(b - 1))
                sp.wait_ge(qkh_ok.sem, qkh_ok.at(b))
                sp.dma_start(qk_d[0].rearrange("(k p) s -> p k s", p=P), qkh).then_inc(hi_out.sem, 16)
                sp.wait_ge(qkl_ok.sem, qkl_ok.at(b))
                sp.dma_start(qk_d[1].rearrange("(k p) s -> p k s", p=P), qkl).then_inc(lo_out.sem, 16)
                if not first(b):
                    sp.wait_ge(st_ps.sem, st_ps.at(b - 1))
                if first(b):
                    sp.wait_ge(zero_ok.sem, zero_ok.at(0))
                sp.wait_ge(hi_out.sem, hi_out.at(b))
                for part, at in ((0, 0), (0, 64), (1, 32)):
                    if part == 1:
                        sp.wait_ge(lo_out.sem, lo_out.at(b))
                    sp.dma_start(qst[at:at + 32, :, :].bitcast(FP32), qk_d[part, 0:D].rearrange("(q r) s -> r q s", r=32)).then_inc(stack_in.sem, 16)
                    for e in range(2):
                        at_k = {(0, 0): 0, (0, 64): 32, (1, 32): 64}[(part, at)] + DH * e
                        sp.dma_start(kst[at_k:at_k + DH, :, :].rearrange("r (q e) s -> r q e s", e=2)[:, :, e, :].bitcast(FP32),
                                     qk_d[part, D:2 * D].rearrange("(q e r) s -> r q e s", e=2, r=DH)[:, :, e, :]).then_inc(stack_in.sem, 16)

            def nrows(b):
                sp.wait_ge(nrow_ok.sem, nrow_ok.at(b))
                for r in range(4):
                    sp.dma_start(qst[96 + r:97 + r, :, :].bitcast(FP32), nrow[r * PAIRS:(r + 1) * PAIRS, :].bitcast(FP32)).then_inc(nrow_in.sem, 16)

            def store(b):
                sp.wait_ge(res_ok.sem, res_ok.at(b))
                sp.dma_start(out[b].rearrange("(c p) d -> p c d", p=P), res[:]).then_inc(res_out.sem, 16)

            get_consts = fetch(consts[:], consts_in, consts_arr)
            get_vec = fetch(vec[:], cols, vec_in)
            get_brow = fetch(b32, rows_in[0:1, D:2 * D].broadcast_to([B, D]), brow_in)
            get_wb = fetch(wb[:], rows_in[0:1, 2 * D:2 * D + L + 1].broadcast_to([P, L + 1]), wb_in)
            get_wc2 = fetch(wc[:, C_W1:], wcond[:, C_W1:], wc2_in)
            get_rope = fetch(rope[:], tabs[:, 0:2 * TC * DH].rearrange("p (a c d) -> p a c d", a=2, c=TC), rope_in)
            get_angles = fetch(angles, tabs[:, 2 * TC * DH:].rearrange("p (a s) -> p a s", a=2), angles_in)
            get_wsm = fetch(wsm[:].rearrange("p a d k n -> p (a d k n)"), wsmall, wsm_in)
            get_bo = fetch(bo[:], rows_in[0:1, 0:D].broadcast_to([P, D]), bo_in)

            def round_(it):
                once(weights("qk", 1), it)
                once(weights("q0", 0), it + 1)
                once(weights("g", 2), it)
                once(weights("u", 2), it)
                once(get_wb, it + 1)
                once(get_brow, it + 1)
                once(weights("u", 0), it)
                once(weights("u", 3), it)
                step(load_adj, it + 1)
                once(cond, it + 1)
                once(weights("self", 0), it + 1)
                once(weights("d", 2), it - 1)
                once(get_wc2, it)
                once(get_consts, it + 1)
                once(weights("g", 3), it)
                step(load_x, it + 1)
                once(weights("u", 1), it)
                once(weights("d", 0), it)
                once(get_rope, it)
                step(load_x_add, it)
                once(weights("q0", 1), it + 1)
                once(weights("v", 0), it + 1)
                once(weights("d", 1), it)
                once(weights("qk", 0), it + 1)
                once(get_vec, it + 1)
                once(weights("d", 3), it - 1)
                once(weights("o", 0), it + 1)
                once(qrows, it + 1)
                once(get_angles, it + 1)
                once(get_bo, it + 1)
                step(load_q, it + 1)
                step(stack, it)
                once(weights("g", 1), it + 1)
                step(nrows, it)
                once(weights("g", 0), it + 1)
                once(get_wsm, it + 1)
                step(store, it - 1)

            rounds(sp, round_, 1, -1)
            sp.wait_ge(res_out.sem, 16 * B)

        @block.gpsimd
        def _(pool):
            def fills():
                pool.memset(nz4[:], 1.0)
                pool.memset(mhalf[:], -0.5)
                pool.memset(prob[:], 0.0)
                pool.memset(vv[:, :, :, DH:], 1.0).then_inc(const_ok.sem, 1)

            def wlow(part, n):
                def step():
                    a = PARTS[part][0] + n * PIECE
                    pool.wait_ge(w_high[part].sem, w_high[part].at(0, n + 1))
                    pool.tensor_tensor(wl[:, a:a + PIECE], slots[PIECES.index((part, n)) % len(slots)], wh[:, a:a + PIECE].bitcast(FP32),
                                       ALU.subtract).then_inc(w_low[part].sem, 1)
                return step

            def low(into, whole, high, signal):
                pool.tensor_tensor(into, whole, high.bitcast(FP32), ALU.subtract).then_inc(signal.sem, 1)

            def selfl(b):
                pool.wait_ge(selfh_ok.sem, selfh_ok.at(b))
                low(splx[:, 1], self32[:], splx[:, 0], selfl_ok)

            def aadd(c):
                def step(b):
                    pool.wait_ge(am_ok.sem, am_ok.at(b, c + 1))
                    pool.wait_ge(msk_ok.sem, msk_ok.at(b))
                    pool.tensor_tensor(aff[:, c], aff[:, c], off[:, :, c, :].unsqueeze(2).broadcast_to([P, 2, H, M]),
                                       ALU.add).then_inc(aa_ok.sem, 1)
                return step

            def asub(c):
                def step(b):
                    pool.wait_ge(amx_ok.sem, amx_ok.at(b, c + 1))
                    t = aff[:, c].rearrange("p d h m -> p (d h) m")
                    pool.tensor_tensor(t, t, amx[:, c, :].unsqueeze(2).broadcast_to([P, 2 * H, M]),
                                       ALU.subtract).then_inc(asub_ok.sem, 1)
                return step

            def aprob(c):
                def step(b):
                    pool.wait_ge(arc_ok.sem, arc_ok.at(b, c + 1))
                    if first(b):
                        pool.wait_ge(const_ok.sem, const_ok.at(0))
                    if c == 0:
                        if not first(b):
                            pool.wait_ge(pT_ps.sem, pT_ps.at(b - 1))
                    else:
                        pool.wait_ge(pT_ps.sem, pT_ps.at(b, 2))
                    pool.tensor_tensor(prob[:, :, 0:M], aff[:, c].rearrange("p d h m -> p (d h) m"),
                                       arc[:, c, :].unsqueeze(2).broadcast_to([P, 2 * H, M]), ALU.mult).then_inc(prob_ok.sem, 1)
                return step

            def pow1(b):
                pool.wait_ge(v1_ok.sem, v1_ok.at(b))
                pool.tensor_tensor(r1[:], v1[:], mhalf[:], ALU.pow).then_inc(r1_ok.sem, 1)

            def nxl(b):
                pool.wait_ge(nxh_ok.sem, nxh_ok.at(b))
                low(sply[:, 1], nx32, sply[:, 0], nxl_ok)

            def x1bias(b):
                pool.wait_ge(x1_ok.sem, x1_ok.at(b))
                if not first(b):
                    pool.wait_ge(x2_ok.sem, x2_ok.at(b - 1))
                if first(b):
                    pool.wait_ge(bo_in.sem, bo_in.at(0))
                if first(b):
                    part, n = last_piece[SLOT_X1B]
                    pool.wait_ge(w_low[part].sem, w_low[part].at(0, n + 1))
                pool.tensor_tensor(x1b[:], x1[:], bo[:].unsqueeze(1).broadcast_to([P, TC, D]), ALU.add).then_inc(x1b_ok.sem, 1)

            def radd(c):
                def step(b):
                    pool.wait_ge(rot_ok.sem, rot_ok.at(b, c + 1))
                    pool.tensor_tensor(t1[:, c], t1[:, c], t2[:, c], ALU.add).then_inc(radd_ok.sem, 1)
                return step

            def qklow(n):
                def step(b):
                    pool.wait_ge(qkh_ok.sem, qkh_ok.at(b, n + 1))
                    pool.tensor_tensor(qkl[:, 2 * n:2 * n + 2].bitcast(F32R), qk32, qkh[:, 2 * n:2 * n + 2],
                                       ALU.subtract).then_inc(qkl_ok.sem, 1)
                return step

            def alow(b):
                pool.wait_ge(ah_ok.sem, ah_ok.at(b))
                low(spla[:, 1], a32, spla[:, 0], al_ok)

            def pow2(b):
                pool.wait_ge(v2_ok.sem, v2_ok.at(b))
                pool.tensor_tensor(r2[:], v2[:], mhalf[:], ALU.pow).then_inc(r2_ok.sem, 1)

            def nzl(b):
                pool.wait_ge(nzh_ok.sem, nzh_ok.at(b))
                low(splz[:, 1], nz32, splz[:, 0], nzl_ok)

            def hlow(j):
                def step(b):
                    pool.wait_ge(hh_ok.sem, hh_ok.at(b, j + 1))
                    low(hs[:, j % 2, 1], g32[:, j % 2], hs[:, j % 2, 0], hl_ok)
                return step

            def round_(it):
                step(asub(1), it)
                once(fills, it + 1)
                step(aprob(1), it)
                once(wlow("g", 1), it)
                once(wlow("d", 2), it - 1)
                once(wlow("g", 2), it)
                step(pow1, it)
                once(wlow("o", 0), it + 1)
                once(wlow("d", 0), it)
                once(wlow("d", 3), it - 1)
                step(alow, it - 1)
                step(nxl, it)
                step(selfl, it + 1)
                step(pow2, it - 1)
                step(radd(0), it)
                step(radd(1), it)
                once(wlow("d", 1), it)
                step(qklow(0), it)
                once(wlow("g", 0), it + 1)
                step(nzl, it - 1)
                step(qklow(1), it)
                step(aadd(0), it + 1)
                once(wlow("g", 3), it)
                step(hlow(0), it - 1)
                step(asub(0), it + 1)
                step(aadd(1), it + 1)
                step(aprob(0), it + 1)
                step(x1bias, it)
                step(hlow(1), it - 1)
                step(hlow(2), it - 1)
                step(hlow(3), it - 1)

            rounds(pool, round_, 1, -1)

        @block.scalar
        def _(act):
            ident_fn = ACT.Identity
            def hidden_cond():
                act.wait_ge(vec_in.sem, vec_in.at(0))
                act.wait_ge(c_ps.sem, c_ps.at(0, 2))
                for n in range(2):
                    for k in range(KC):
                        at = 2 * n + k
                        ins = act.activation(hT[:, n, k, :], ps[:, 1, at * B:(at + 1) * B], ACT.Silu, bias=vec[:, V_B1 + at:V_B1 + at + 1])
                ins.then_inc(h_ok.sem, 1)

            def whigh(part, n):
                def step():
                    a = PARTS[part][0] + n * PIECE
                    at = PIECES.index((part, n))
                    act.wait_ge(w_in[at % len(slots)].sem, w_in[at % len(slots)].at(at // len(slots)))
                    act.activation(wh[:, a:a + PIECE], slots[at % len(slots)], ACT.Copy).then_inc(w_high[part].sem, 1)
                return step

            def xh(b):
                act.wait_ge(xT_ps.sem, xT_ps.at(b))
                if not first(b):
                    act.wait_ge(q0_ps.sem, q0_ps.at(b - 1))
                act.activation(splx[:, 0], ps[:, BANK["xT"]].rearrange("p (k s) -> p k s", k=KC), ACT.Copy).then_inc(xh_ok.sem, 1)

            def nzt(b):
                act.wait_ge(nzT_ps.sem, nzT_ps.at(b))
                if not first(b):
                    act.wait_ge(self_ps.sem, self_ps.at(b - 1))
                act.activation(nzT[:], ps[0:4, BANK["nzT"], 0:S], ACT.Copy).then_inc(nzT_ok.sem, 1)

            def selfc(b):
                act.wait_ge(self_ps.sem, self_ps.at(b))
                if not first(b):
                    act.wait_ge(y_ok.sem, y_ok.at(b - 1))
                act.activation(self32[:], ps[:, BANK["self"]].rearrange("p (k s) -> p k s", k=KC), ACT.Copy).then_inc(self_ok.sem, 1)

            def kvrep(b):
                act.wait_ge(self_ok.sem, self_ok.at(b))
                if not first(b):
                    act.wait_ge(v0_ps.sem, v0_ps.at(b - 1))
                act.activation(kvr[:], self32[:, :, 0:MP].unsqueeze(2).broadcast_to([P, KC, 4, MP]), ACT.Copy).then_inc(kvr_ok.sem, 1)

            def q0c(d):
                def step(b):
                    act.wait_ge(q0_ps.sem, q0_ps.at(b, 2 * d + 2))
                    if first(b):
                        act.wait_ge(vec_in.sem, vec_in.at(0))
                    for k in range(KC):
                        at = V_BQ0 + 2 * d + k
                        ins = act.activation(q0T[:, d, k, :], ps[:, BANK["q0"][d], k * S:(k + 1) * S], ident_fn, bias=vec[:, at:at + 1])
                    ins.then_inc(q0T_ok.sem, 1)
                return step

            def aexp(c):
                def step(b):
                    act.wait_ge(asub_ok.sem, asub_ok.at(b, c + 1))
                    act.activation(aff[:, c], aff[:, c], ACT.Exp).then_inc(aexp_ok.sem, 1)
                return step

            def square1(b):
                act.wait_ge(x1_ok.sem, x1_ok.at(b))
                if not first(b):
                    act.wait_ge(nxl_ok.sem, nxl_ok.at(b - 1))
                if first(b):
                    part, n = last_piece[SLOT_XR]
                    act.wait_ge(w_low[part].sem, w_low[part].at(0, n + 1))
                for c in range(TC):
                    ins = act.activation(xr[:, c], x1[:, c], ACT.Square, accum_out=ss1[:, c:c + 1])
                    ins.then_inc(ss1_ok.sem, 1)

            def nxc(b):
                act.wait_ge(nx_ps.sem, nx_ps.at(b))
                act.wait_ge(cur1_ok.sem, cur1_ok.at(b))
                for k in range(KC):
                    ins = act.activation(nx32[:, k, :], ps[:, BANK["nx"], k * S:(k + 1) * S], ident_fn,
                                         scale=cur1[:, k:k + 1], bias=cur1[:, 2 + k:3 + k])
                ins.then_inc(nx_ok.sem, 1)

            def vcopy(b):
                act.wait_ge(v_ps.sem, v_ps.at(b))
                if not first(b):
                    act.wait_ge(pv_ps.sem, pv_ps.at(b - 1))
                if first(b):
                    act.wait_ge(const_ok.sem, const_ok.at(0))
                act.activation(vv[:, :, :, 0:DH], ps[:, BANK["v"]].rearrange("p (c h d) -> p c h d", c=TC, h=H), ACT.Copy).then_inc(vv_ok.sem, 1)

            def nrowc(b):
                act.wait_ge(nmT_ps.sem, nmT_ps.at(b))
                if not first(b):
                    act.wait_ge(nrow_in.sem, nrow_in.at(b - 1))
                act.activation(nrow[:], ps[0:4 * PAIRS, BANK["nmT"], 0:S], ACT.Copy).then_inc(nrow_ok.sem, 1)

            def exph(h):
                def step(b):
                    act.wait_ge(st_ps.sem, st_ps.at(b, h + 1))
                    if h == 0:
                        act.wait_ge(hi_out.sem, hi_out.at(b))
                        act.wait_ge(lo_out.sem, lo_out.at(b))
                    if h >= EXR:
                        act.wait_ge(pv_ps.sem, pv_ps.at(b, (h - EXR) // 4 + 1))
                    act.activation(ex[:, h % EXR], ps[:, h % 2].rearrange("p (c s) -> p c s", c=TC), ACT.Exp, scale=SCALE).then_inc(ex_ok.sem, 1)
                return step

            def oc(n):
                def step(b):
                    act.wait_ge(pv_ps.sem, pv_ps.at(b, 2 * n + 2))
                    act.activation(oT32[:, 2 * n:2 * n + 2, :], ps[:, 2].rearrange("p (g s) -> p g s", g=2), ACT.Copy).then_inc(o_ok.sem, 1)
                return step

            def square2(b):
                act.wait_ge(x2_ok.sem, x2_ok.at(b))
                if not first(b):
                    act.wait_ge(res_out.sem, res_out.at(b - 1))
                if first(b):
                    part, n = last_piece[SLOT_XR2]
                    act.wait_ge(w_low[part].sem, w_low[part].at(0, n + 1))
                for c in range(TC):
                    act.activation(xr2[:, c], x2[:, c], ACT.Square, accum_out=ss2[:, c:c + 1]).then_inc(ss2_ok.sem, 1)

            def nzc(b):
                act.wait_ge(nz_ps.sem, nz_ps.at(b))
                act.wait_ge(cur2_ok.sem, cur2_ok.at(b))
                if not first(b):
                    act.wait_ge(hl_ok.sem, hl_ok.at(b - 1))
                for k in range(KC):
                    ins = act.activation(nz32[:, k, :], ps[:, BANK["nz"], k * S:(k + 1) * S], ident_fn,
                                         scale=cur2[:, k:k + 1], bias=cur2[:, 2 + k:3 + k])
                ins.then_inc(nz_sb.sem, 1)

            def gelu(j):
                def step(b):
                    act.wait_ge(g_ps.sem, g_ps.at(b, 2 * j + 2))
                    if j >= 2:
                        act.wait_ge(hl_ok.sem, hl_ok.at(b, j - 1))
                    else:
                        if not first(b):
                            act.wait_ge(hl_ok.sem, hl_ok.at(b - 1, NJ - 1 + j))
                    act.activation(g32[:, j % 2], ps[:, BANK["g"]].rearrange("p (k s) -> p k s", k=2), ACT.Gelu).then_inc(gelu_ok.sem, 1)
                return step

            def round_(it):
                step(exph(0), it - 1)
                step(exph(1), it - 1)
                once(whigh("u", 2), it)
                once(whigh("qk", 0), it + 1)
                once(whigh("self", 0), it + 1)
                step(exph(2), it - 1)
                step(exph(3), it - 1)
                once(hidden_cond, it)
                step(exph(4), it - 1)
                step(exph(5), it - 1)
                step(exph(6), it - 1)
                step(exph(7), it - 1)
                once(whigh("g", 2), it)
                step(exph(8), it - 1)
                step(exph(9), it - 1)
                step(exph(10), it - 1)
                step(exph(11), it - 1)
                once(whigh("d", 2), it - 1)
                step(oc(0), it - 1)
                step(exph(12), it - 1)
                once(whigh("d", 0), it)
                step(exph(13), it - 1)
                once(whigh("g", 3), it)
                step(exph(14), it - 1)
                once(whigh("q0", 0), it + 1)
                once(whigh("u", 3), it)
                step(exph(15), it - 1)
                once(whigh("o", 0), it + 1)
                step(oc(1), it - 1)
                step(square1, it)
                once(whigh("d", 3), it - 1)
                step(xh, it + 1)
                step(nzt, it + 1)
                once(whigh("q0", 1), it + 1)
                once(whigh("d", 1), it)
                step(nxc, it)
                step(selfc, it + 1)
                step(square2, it - 1)
                step(vcopy, it)
                once(whigh("qk", 1), it + 1)
                step(kvrep, it + 1)
                once(whigh("v", 0), it + 1)
                once(whigh("g", 0), it + 1)
                step(q0c(0), it + 1)
                step(nzc, it - 1)
                step(q0c(1), it + 1)
                step(gelu(0), it - 1)
                step(gelu(1), it - 1)
                once(whigh("g", 1), it + 1)
                step(aexp(0), it + 1)
                step(gelu(2), it - 1)
                step(gelu(3), it - 1)
                once(whigh("u", 0), it + 1)
                once(whigh("u", 1), it + 1)
                step(nrowc, it)
                step(aexp(1), it + 1)

            rounds(act, round_, 1, -1)

        @block.vector
        def _(dve):
            def high(into, whole, signal):
                dve.tensor_copy(into, whole).then_inc(signal.sem, 1)

            def zeros(n):
                def step():
                    dve.memset(kst[0:96, n * H // 2:(n + 1) * H // 2, :].bitcast(FP32), 0.0).then_inc(zero_ok.sem, 1)
                return step

            def ones(n):
                def step():
                    dve.wait_ge(consts_arr.sem, consts_arr.at(0))
                    dve.tensor_copy(kst[96:100, n * H // 2:(n + 1) * H // 2, :],
                                    consts[96:100, K_ONES + n * H // 2:K_ONES + (n + 1) * H // 2].unsqueeze(2).broadcast_to([4, H // 2, S])
                                    ).then_inc(ones_ok.sem, 1)
                return step

            def qrow_parts():
                dve.wait_ge(brow_in.sem, brow_in.at(0))
                dve.tensor_copy(qrow[:, 2, :], b32)
                dve.wait_ge(c_ps.sem, c_ps.at(0, 1))
                dve.tensor_copy(q32, ps[0:B, 0, 0:D]).then_inc(c_sb.sem, 1)
                dve.wait_ge(c_sb.sem, c_sb.at(0, 1))
                dve.tensor_copy(qrow[:, 0, :], q32).then_inc(c_sb.sem, 1)
                dve.wait_ge(c_sb.sem, c_sb.at(0, 2))
                dve.tensor_tensor(qrow[:, 1, :], q32, qrow[:, 0, :].bitcast(FP32), ALU.subtract)
                dve.tensor_tensor(qrow[:, 3, :], b32, qrow[:, 2, :].bitcast(FP32), ALU.subtract).then_inc(qrow_ok.sem, 1)

            def bout():
                dve.wait_ge(vec_in.sem, vec_in.at(0))
                dve.tensor_tensor(vec[:, V_BOUT:V_BOUT + 2], vec[:, V_BOUT:V_BOUT + 2], vec[:, V_BOUT + 2:V_BOUT + 4], ALU.add).then_inc(bout_ok.sem, 1)

            def rotated_bias():
                dve.wait_ge(vec_in.sem, vec_in.at(0))
                dve.wait_ge(angles_in.sem, angles_in.at(0))
                for k in range(2 * KC):
                    dve.tensor_scalar(rbT[:, k, :], angles[:, 0, :], vec[:, V_BQK + k:V_BQK + k + 1], None, ALU.mult).then_inc(rb_ok.sem, 1)
                dve.wait_ge(rb_ok.sem, rb_ok.at(0, 2 * KC))
                for k in range(2 * KC):
                    dve.scalar_tensor_tensor(out=rbT[:, k, :], in0=angles[:, 1, :], scalar=vec[:, V_BQKS + k:V_BQKS + k + 1],
                                             in1=rbT[:, k, :], op0=ALU.mult, op1=ALU.add).then_inc(rb_ok.sem, 1)

            def wlow(part, n):
                def step():
                    a = PARTS[part][0] + n * PIECE
                    dve.wait_ge(w_high[part].sem, w_high[part].at(0, n + 1))
                    dve.tensor_tensor(wl[:, a:a + PIECE], slots[PIECES.index((part, n)) % len(slots)], wh[:, a:a + PIECE].bitcast(FP32),
                                      ALU.subtract).then_inc(w_low[part].sem, 1)
                return step

            def table():
                dve.wait_ge(vec_in.sem, vec_in.at(0))
                dve.wait_ge(c_ps.sem, c_ps.at(0))
                cc = ps[:, 1, 64:64 + 8 * B].rearrange("p (n a k b) -> p n a k b", n=2, a=2, k=KC)
                for n in range(2):
                    for k in range(KC):
                        at = V_B2 + 4 * n + k
                        dve.tensor_scalar(tab[:, n, :, 2 + k], cc[:, n, 1, k, :], vec[:, at + 2:at + 3], None, ALU.add)
                        dve.tensor_scalar(tab[:, n, :, k], cc[:, n, 0, k, :], vec[:, at:at + 1], 1.0, ALU.add, ALU.add).then_inc(tab_ok.sem, 1)
                dve.wait_ge(tab_ok.sem, tab_ok.at(0, 4))
                for n in range(2):
                    for k in range(KC):
                        dve.tensor_scalar(tab[:, n, :, k], tab[:, n, :, k], vec[:, V_WN + 2 * n + k:V_WN + 2 * n + k + 1], None,
                                          ALU.mult).then_inc(tab_ok.sem, 1)

            def adjm(b):
                dve.wait_ge(adj_in.sem, adj_in.at(b))
                if not first(b):
                    dve.wait_ge(prob_ok.sem, prob_ok.at(b - 1))
                if first(b):
                    dve.wait_ge(wb_in.sem, wb_in.at(0))
                r = adjR[:].rearrange("p (n l) -> p n l", l=L)
                c = adjC[:].rearrange("p (n l) -> p n l", l=L)
                pr, pc = prodR.rearrange("p (n l) -> p n l", l=L), prodC.rearrange("p (n l) -> p n l", l=L)
                flat = cw[:].rearrange("p a d c m -> p a d (c m)")
                dve.tensor_tensor(pc, c, wb[0:AQ * M, 0:L].unsqueeze(1).broadcast_to([AQ * M, AN, L]), ALU.mult)
                dve.tensor_tensor(pr, r, wb[:, 0:L].unsqueeze(1).broadcast_to([P, TC * M, L]), ALU.mult).then_inc(prod_ok.sem, 1)
                if not first(b):
                    dve.wait_ge(adjT_ps.sem, adjT_ps.at(b - 1))
                dve.tensor_reduce(cwC[:, 0, :], c, AX.X, ALU.add)
                dve.tensor_reduce(flat[:, 0, 0, :], r, AX.X, ALU.add)
                dve.wait_ge(prod_ok.sem, prod_ok.at(b))
                dve.tensor_reduce(cwC[:, 1, :], pc, AX.X, ALU.add)
                dve.tensor_reduce(flat[:, 1, 0, :], pr, AX.X, ALU.add).then_inc(adj_ok.sem, 1)

            def mask(b):
                dve.wait_ge(adjT_ps.sem, adjT_ps.at(b))
                dve.tensor_copy(cw[:, :, 1].rearrange("p a c m -> p a (c m)"),
                                ps[:, BANK["adjT"], 0:4 * M].rearrange("p (a n) -> p a n", a=2)).then_inc(cw_ok.sem, 1)
                dve.wait_ge(cw_ok.sem, cw_ok.at(b))
                dve.wait_ge(adj_ok.sem, adj_ok.at(b))
                if not first(b):
                    dve.wait_ge(aa_ok.sem, aa_ok.at(b - 1))
                cnt, ws = (cw[:, a].rearrange("p d c m -> p (d c m)") for a in range(2))
                mf, of = msk[:].rearrange("p d c m -> p (d c m)"), off[:].rearrange("p d c m -> p (d c m)")
                dve.tensor_scalar(mf, cnt, 0.0, SCALE, ALU.is_gt, ALU.mult)
                dve.tensor_scalar(of, cnt, 0.0, NEG, ALU.is_le, ALU.mult).then_inc(off_ok.sem, 1)
                dve.wait_ge(off_ok.sem, off_ok.at(b))
                dve.scalar_tensor_tensor(out=of, in0=ws, scalar=wb[:, L:L + 1], in1=of, op0=ALU.add, op1=ALU.add).then_inc(msk_ok.sem, 1)

            def nz(b):
                dve.wait_ge(x_in.sem, x_in.at(b))
                dve.tensor_reduce(rs[:], x_tok[:], AX.X, ALU.add).then_inc(rs_ok.sem, 1)
                dve.wait_ge(rs_ok.sem, rs_ok.at(b))
                if first(b):
                    dve.wait_ge(const_ok.sem, const_ok.at(0))
                if not first(b):
                    dve.wait_ge(nzT_ps.sem, nzT_ps.at(b - 1))
                dve.tensor_scalar(nz4[:, :, 0:2], rs[:].unsqueeze(2).broadcast_to([P, TC, 2]), 0.0, None, ALU.not_equal).then_inc(nz_ok.sem, 1)

            def xl(b):
                dve.wait_ge(xh_ok.sem, xh_ok.at(b))
                dve.tensor_tensor(splx[:, 1], ps[:, BANK["xT"]].rearrange("p (k s) -> p k s", k=KC), splx[:, 0].bitcast(FP32),
                                  ALU.subtract).then_inc(xl_ok.sem, 1)

            def selfh(b):
                dve.wait_ge(self_ok.sem, self_ok.at(b))
                high(splx[:, 0], self32[:], selfh_ok)

            def kb(b):
                dve.wait_ge(k0_ps.sem, k0_ps.at(b))
                if first(b):
                    dve.wait_ge(vec_in.sem, vec_in.at(0))
                if first(b):
                    dve.wait_ge(consts_arr.sem, consts_arr.at(0))
                for d in range(2):
                    for k in range(KC):
                        at = V_BK0 + 2 * d + k
                        src = ps[:, BANK["k0"], (2 * d + k) * KN:(2 * d + k) * KN + M]
                        ins = dve.scalar_tensor_tensor(
                            out=kblk[:, d, k], in0=src.unsqueeze(1).broadcast_to([P, 8, M]), scalar=vec[:, at:at + 1],
                            in1=mask8.unsqueeze(2).broadcast_to([P, 8, M]), op0=ALU.add, op1=ALU.mult)
                ins.then_inc(kblk_ok.sem, 1)

            def am(c):
                def step(b):
                    dve.wait_ge(aff_ps.sem, aff_ps.at(b, c + 1))
                    dve.wait_ge(msk_ok.sem, msk_ok.at(b))
                    dve.tensor_tensor(aff[:, c], ps[:, 3:5, 0:H * M].rearrange("p d (h m) -> p d h m", h=H),
                                      msk[:, :, c, :].unsqueeze(2).broadcast_to([P, 2, H, M]), ALU.mult).then_inc(am_ok.sem, 1)
                return step

            def amax(c):
                def step(b):
                    dve.wait_ge(aa_ok.sem, aa_ok.at(b, c + 1))
                    dve.tensor_reduce(amx[:, c, :], aff[:, c].rearrange("p d h m -> p (d h) m"), AX.X, ALU.max).then_inc(amx_ok.sem, 1)
                return step

            def pTc(n):
                def step(b):
                    c, d = divmod(n, 2)
                    dve.wait_ge(pT_ps.sem, pT_ps.at(b, n + 1))
                    dve.tensor_copy(pT[:, d, :, c * P:(c + 1) * P], ps[:, BANK["pT"][n % 2]].rearrange("p (g s) -> p g s", g=4)
                                    ).then_inc(pT_ok.sem, 1)
                return step

            def asums(c):
                def step(b):
                    dve.wait_ge(aexp_ok.sem, aexp_ok.at(b, c + 1))
                    dve.tensor_reduce(asum[:, c, :], aff[:, c].rearrange("p d h m -> p (d h) m"), AX.X, ALU.add).then_inc(asum_ok.sem, 1)
                    dve.wait_ge(asum_ok.sem, asum_ok.at(b, c + 1))
                    dve.reciprocal(arc[:, c, :], asum[:, c, :]).then_inc(arc_ok.sem, 1)
                return step

            def vb(b):
                dve.wait_ge(v0_ps.sem, v0_ps.at(b))
                if not first(b):
                    dve.wait_ge(y_ps.sem, y_ps.at(b - 1))
                if first(b):
                    dve.wait_ge(consts_arr.sem, consts_arr.at(0))
                dve.tensor_tensor(vblk[:].rearrange("p d g (h n) -> p (d g) h n", h=4),
                                  ps[:, BANK["v0"]].rearrange("p (g h n) -> p g h n", h=4, n=DH),
                                  mask4.unsqueeze(1).unsqueeze(3).broadcast_to([P, 8, 4, DH]), ALU.mult).then_inc(vblk_ok.sem, 1)

            def yadd(b):
                dve.wait_ge(y_ps.sem, y_ps.at(b))
                if first(b):
                    dve.wait_ge(bout_ok.sem, bout_ok.at(0))
                dve.tensor_tensor(yT, ps[:, BANK["y"]].rearrange("p (k s) -> p k s", k=KC), self32[:], ALU.add).then_inc(y_ok.sem, 1)
                dve.wait_ge(y_ok.sem, y_ok.at(b))
                for k in range(KC):
                    ins = dve.tensor_scalar(yT[:, k, :], yT[:, k, :], vec[:, V_BOUT + k:V_BOUT + k + 1], 0.0, ALU.add, ALU.max)
                ins.then_inc(yr_ok.sem, 1)

            def x1add(b):
                dve.wait_ge(x1_ps.sem, x1_ps.at(b))
                dve.wait_ge(xa_in.sem, xa_in.at(b))
                if not first(b):
                    dve.wait_ge(xr_ok.sem, xr_ok.at(b - 1))
                if not first(b):
                    dve.wait_ge(x1b_ok.sem, x1b_ok.at(b - 1))
                dve.tensor_tensor(x1[:], ps[:, BANK["x1"]].rearrange("p (c d) -> p c d", c=TC), x_add[:], ALU.add).then_inc(x1_ok.sem, 1)

            def norm_in(ss, v, ss_ok, v_ok):
                def step(b):
                    dve.wait_ge(ss_ok.sem, ss_ok.at(b))
                    dve.tensor_scalar(v[:], ss[:], 1.0 / D, EPS, ALU.mult, ALU.add).then_inc(v_ok.sem, 1)
                return step

            def cur(n, now, ok, used):
                def step(b):
                    if not first(b):
                        dve.wait_ge(used.sem, used.at(b - 1))
                    if first(b):
                        dve.wait_ge(tab_ok.sem, tab_ok.at(0))
                    dve.tensor_copy(now[:], tab[:, n, bass.ds(b, 1), :].rearrange("p b n -> p (b n)")).then_inc(ok.sem, 1)
                return step

            def scaled(src, dst, r, r_ok, ok):
                def step(b):
                    dve.wait_ge(r_ok.sem, r_ok.at(b))
                    for c in range(TC):
                        ins = dve.tensor_scalar(dst[:, c], src[:, c], r[:, c:c + 1], None, ALU.mult)
                    ins.then_inc(ok.sem, 1)
                return step

            def nxh(b):
                dve.wait_ge(nx_ok.sem, nx_ok.at(b))
                if not first(b):
                    dve.wait_ge(v_ps.sem, v_ps.at(b - 1))
                high(sply[:, 0], nx32, nxh_ok)

            def rot(c):
                def step(b):
                    dve.wait_ge(qk_ps.sem, qk_ps.at(b, c + 1))
                    if not first(b):
                        dve.wait_ge(pv_ps.sem, pv_ps.at(b - 1))
                    else:
                        dve.wait_ge(c_ps.sem, c_ps.at(0))
                    if first(b):
                        dve.wait_ge(rope_in.sem, rope_in.at(0))
                    src = ps[:, BANK["qk"][c]].rearrange("p (h a d) -> p h a d", a=2, d=DH // 2)
                    cs, sn = (rope[:, i, c, :].rearrange("p (a d) -> p a d", a=2).unsqueeze(1).broadcast_to([P, 2 * H, 2, DH // 2]) for i in range(2))
                    dve.tensor_tensor(t1[:, c].rearrange("p (h a d) -> p h a d", a=2, d=DH // 2), src, cs, ALU.mult)
                    dve.tensor_tensor(t2[:, c].rearrange("p (h a d) -> p h a d", a=2, d=DH // 2), src[:, :, ::-1, :], sn, ALU.mult).then_inc(rot_ok.sem, 1)
                return step

            def qkadd(n):
                def step(b):
                    dve.wait_ge(qkT_ps.sem, qkT_ps.at(b, n + 1))
                    if first(b):
                        dve.wait_ge(rb_ok.sem, rb_ok.at(0))
                    if first(b):
                        for part, last in (last_piece[slot] for slot in SLOTS_YA):
                            dve.wait_ge(w_low[part].sem, w_low[part].at(0, last + 1))
                    if n:
                        dve.wait_ge(qkl_ok.sem, qkl_ok.at(b, n))
                    elif not first(b):
                        dve.wait_ge(al_ok.sem, al_ok.at(b - 1))
                    dve.tensor_tensor(qk32, ps[:, BANK["qkT"][n]].rearrange("p (k s) -> p k s", k=KC), rbT[:, 2 * n:2 * n + 2, :],
                                      ALU.add).then_inc(qk_ok.sem, 1)
                    dve.wait_ge(qk_ok.sem, qk_ok.at(b, n + 1))
                    dve.tensor_copy(qkh[:, 2 * n:2 * n + 2].bitcast(F32R), qk32).then_inc(qkh_ok.sem, 1)
                return step

            def mx(h):
                def step(b):
                    dve.wait_ge(s_ps.sem, s_ps.at(b, h + 1))
                    if h == 0:
                        if not first(b):
                            dve.wait_ge(nm4_ok.sem, nm4_ok.at(b - 1))
                    dve.tensor_reduce(nm[:, :, h], ps[:, h % 2].rearrange("p (c s) -> p c s", c=TC), AX.X, ALU.max, negate=True).then_inc(mx_ok.sem, 1)
                return step

            def nmx(b):
                dve.wait_ge(mx_ok.sem, mx_ok.at(b))
                if not first(b):
                    dve.wait_ge(nmT_ps.sem, nmT_ps.at(b - 1))
                src = nm[:].rearrange("p c (q e) -> p c e q", e=2)
                for c in range(TC):
                    ins = dve.tensor_copy(nm4[:, c, :, 0, :], src[:, c])
                ins.then_inc(nmh_ok.sem, 1)
                dve.wait_ge(nmh_ok.sem, nmh_ok.at(b))
                for c in range(TC):
                    ins = dve.tensor_tensor(nm4[:, c, :, 1, :], src[:, c], nm4[:, c, :, 0, :].bitcast(FP32), ALU.subtract)
                ins.then_inc(nm4_ok.sem, 1)

            def onorm(c):
                def step(b):
                    dve.wait_ge(oT_ps.sem, oT_ps.at(b, c + 1))
                    src = ps[:, BANK["oT"][c]].rearrange("p (h n) -> p h n", h=H)
                    dve.reciprocal(orc[:, c, :], src[:, :, DH]).then_inc(orc_ok.sem, 1)
                    dve.wait_ge(orc_ok.sem, orc_ok.at(b, c + 1))
                    dve.tensor_tensor(attn[:, c].rearrange("p (h n) -> p h n", h=H), src[:, :, 0:DH],
                                      orc[:, c, :].unsqueeze(2).broadcast_to([P, H, DH]), ALU.mult).then_inc(at_ok.sem, 1)
                return step

            def aadd32(b):
                dve.wait_ge(aT_ps.sem, aT_ps.at(b))
                dve.tensor_tensor(a32, ps[:, BANK["aT"]].rearrange("p (k s) -> p k s", k=KC),
                                  vec[:, V_BV:V_BV + 2].unsqueeze(2).broadcast_to([P, KC, S]), ALU.add).then_inc(a_ok.sem, 1)
                dve.wait_ge(a_ok.sem, a_ok.at(b))
                if not first(b):
                    dve.wait_ge(u_ps.sem, u_ps.at(b - 1))
                high(spla[:, 0], a32, ah_ok)

            def x2add(b):
                dve.wait_ge(wo_ps.sem, wo_ps.at(b))
                dve.wait_ge(x1b_ok.sem, x1b_ok.at(b))
                if first(b):
                    part, n = last_piece[SLOT_X2]
                    dve.wait_ge(w_low[part].sem, w_low[part].at(0, n + 1))
                dve.tensor_tensor(x2[:], ps[:, BANK["wo"]].rearrange("p (c d) -> p c d", c=TC), x1b[:], ALU.add).then_inc(x2_ok.sem, 1)

            def nzh(b):
                dve.wait_ge(nz_sb.sem, nz_sb.at(b))
                high(splz[:, 0], nz32, nzh_ok)

            def hmul(j):
                def step(b):
                    dve.wait_ge(gelu_ok.sem, gelu_ok.at(b, j + 1))
                    dve.wait_ge(u_ps.sem, u_ps.at(b, 2 * j + 2))
                    g = g32[:, j % 2]
                    dve.tensor_tensor(g, ps[:, BANK["u"]].rearrange("p (k s) -> p k s", k=2), g, ALU.mult).then_inc(hm_ok.sem, 1)
                    dve.wait_ge(hm_ok.sem, hm_ok.at(b, j + 1))
                    if j >= 2:
                        dve.wait_ge(d_ps.sem, d_ps.at(b, TC * (j - 1)))
                    else:
                        if not first(b):
                            dve.wait_ge(d_ps.sem, d_ps.at(b - 1, TC * (NJ - 1 + j)))
                    high(hs[:, j % 2, 0], g, hh_ok)
                return step

            def result(b):
                dve.wait_ge(d_ps.sem, d_ps.at(b))
                dve.tensor_tensor(res[:], ps[:, BANK["d"]].rearrange("p (c d) -> p c d", c=TC), x2[:], ALU.add).then_inc(res_ok.sem, 1)

            v1_in, v2_in = norm_in(ss1, v1, ss1_ok, v1_ok), norm_in(ss2, v2, ss2_ok, v2_ok)
            cur_1, cur_2 = cur(0, cur1, cur1_ok, nx_ok), cur(1, cur2, cur2_ok, nz_sb)
            xr_scaled, xr2_scaled = scaled(x1, xr, r1, r1_ok, xr_ok), scaled(x2, xr2, r2, r2_ok, xr2_ok)

            def round_(it):
                step(asums(1), it)
                step(pTc(0), it)
                step(pTc(1), it)
                once(wlow("u", 2), it)
                step(pTc(2), it)
                step(pTc(3), it)
                step(adjm, it + 1)
                once(qrow_parts, it + 1)
                once(wlow("u", 3), it)
                step(yadd, it)
                step(nz, it + 1)
                once(wlow("q0", 0), it + 1)
                step(x1add, it)
                once(zeros(1), it)
                step(onorm(0), it - 1)
                step(v1_in, it)
                step(onorm(1), it - 1)
                step(xl, it + 1)
                once(wlow("self", 0), it + 1)
                step(xr_scaled, it)
                step(aadd32, it - 1)
                once(table, it)
                once(wlow("q0", 1), it + 1)
                step(cur_1, it)
                once(zeros(0), it + 1)
                step(nxh, it)
                once(rotated_bias, it)
                step(x2add, it - 1)
                step(selfh, it + 1)
                step(v2_in, it - 1)
                step(rot(0), it)
                step(rot(1), it)
                step(mask, it + 1)
                step(xr2_scaled, it - 1)
                once(wlow("qk", 0), it + 1)
                step(qkadd(0), it)
                step(nzh, it - 1)
                once(ones(1), it)
                once(ones(0), it + 1)
                step(qkadd(1), it)
                step(cur_2, it)
                once(wlow("qk", 1), it + 1)
                step(kb, it + 1)
                once(wlow("v", 0), it + 1)
                once(bout, it + 1)
                step(am(0), it + 1)
                step(hmul(0), it - 1)
                step(amax(0), it + 1)
                step(am(1), it + 1)
                step(hmul(1), it - 1)
                step(asums(0), it + 1)
                step(mx(0), it)
                step(mx(1), it)
                step(mx(2), it)
                step(mx(3), it)
                step(mx(4), it)
                step(mx(5), it)
                step(mx(6), it)
                step(mx(7), it)
                step(hmul(2), it - 1)
                step(mx(8), it)
                step(mx(9), it)
                once(wlow("u", 0), it + 1)
                step(mx(10), it)
                step(mx(11), it)
                step(mx(12), it)
                step(mx(13), it)
                step(mx(14), it)
                step(mx(15), it)
                step(nmx, it)
                step(amax(1), it + 1)
                step(hmul(3), it - 1)
                step(vb, it + 1)
                step(result, it - 1)
                once(wlow("u", 1), it + 1)

            rounds(dve, round_, 1, -1)

        @block.tensor
        def _(pe):
            def product(dst, lhs, rhs, ks, first_=True, last_=True, **kw):
                for n, k in enumerate(ks):
                    for m, (a, c) in enumerate(((0, 0), (0, 1), (1, 0))):
                        ins = pe.matmul(dst, lhs(a, k), rhs(c, k), start=first_ and n == 0 and m == 0,
                                        stop=last_ and n == len(ks) - 1 and m == 2, **kw)
                return ins

            def w(part, base, k, width, a, z):
                t = (wh, wl)[part]
                return t[:, base + k * width + a:base + k * width + z]

            def cond_q():
                pe.wait_ge(cond_in.sem, cond_in.at(0))
                for k in range(KC):
                    ins = pe.matmul(ps[0:B, 0, 0:D], cT[:, k, :], wc[:, C_Q + k * D:C_Q + (k + 1) * D], start=k == 0, stop=k == KC - 1)
                ins.then_inc(c_ps.sem, 1)

            def cond_1():
                pe.wait_ge(cond_in.sem, cond_in.at(0))
                pe.wait_ge(wc2_in.sem, wc2_in.at(0))
                for n in range(2):
                    for o in range(KC):
                        for k in range(KC):
                            at = C_W1 + (n * KC + k) * D + o * P
                            ins = pe.matmul(ps[:, 1, (2 * n + o) * B:(2 * n + o + 1) * B], wc[:, at:at + P], cT[:, k, :], start=k == 0, stop=k == KC - 1)
                ins.then_inc(c_ps.sem, 1)

            def cond_2():
                pe.wait_ge(h_ok.sem, h_ok.at(0))
                for n in range(2):
                    for o in range(4):
                        for k in range(KC):
                            at = C_W2 + (n * KC + k) * 2 * D + o * P
                            ins = pe.matmul(ps[:, 1, 64 + (4 * n + o) * B:64 + (4 * n + o + 1) * B], wc[:, at:at + P], hT[:, n, k, :],
                                            start=k == 0, stop=k == KC - 1)
                ins.then_inc(c_ps.sem, 1)

            def transposes(dst, src, signal):
                for i in range(2):
                    for j in range(2):
                        ins = pe.transpose(dst[:, i * S + j * P:i * S + (j + 1) * P], src(i, j), ident)
                ins.then_inc(signal.sem, 1)

            def xT(b):
                bk = BANK["xT"]
                if not first(b):
                    pe.wait_ge(x1_ok.sem, x1_ok.at(b - 1))
                pe.wait_ge(x_in.sem, x_in.at(b))
                if first(b):
                    pe.wait_ge(consts_arr.sem, consts_arr.at(0))
                transposes(ps[:, bk], lambda k, c: x_tok[:, c, k * P:(k + 1) * P], xT_ps)

            def nzTt(b):
                bk = BANK["nzT"]
                if not first(b):
                    pe.wait_ge(y_ok.sem, y_ok.at(b - 1))
                if first(b):
                    pe.wait_ge(consts_arr.sem, consts_arr.at(0))
                pe.wait_ge(nz_ok.sem, nz_ok.at(b))
                for c in range(TC):
                    ins = pe.transpose(ps[0:4, bk, c * P:(c + 1) * P], nz4[:, c, :], ident)
                ins.then_inc(nzT_ps.sem, 1)

            def selfm(o):
                def step(b):
                    bk = BANK["self"]
                    pe.wait_ge(xl_ok.sem, xl_ok.at(b))
                    if first(b):
                        pe.wait_ge(w_low["self"].sem, w_low["self"].at(0))
                    dst = ps[:, bk, o * S:(o + 1) * S]
                    product(dst, lambda a, k: w(a, W_SELF, k, D, o * P, (o + 1) * P), lambda a, k: splx[:, a, k, :], range(KC), last_=False)
                    pe.wait_ge(nzT_ok.sem, nzT_ok.at(b))
                    pe.wait_ge(q4_in.sem, q4_in.at(b))
                    pe.matmul(dst, q4[:, o * P:(o + 1) * P], nzT[:], start=False, stop=True).then_inc(self_ps.sem, 1)
                return step

            def adjT(b):
                bk = BANK["adjT"]
                pe.wait_ge(nzT_ok.sem, nzT_ok.at(b))
                pe.wait_ge(adj_ok.sem, adj_ok.at(b))
                for a in range(2):
                    for j in range(2):
                        ins = pe.matmul(ps[64 * j:64 * j + 64, bk, a * 2 * M:(a + 1) * 2 * M], cwC[:, a, :],
                                        sel[:, j].rearrange("p n m -> p (n m)"), start=True, stop=True)
                ins.then_inc(adjT_ps.sem, 1)

            def q0(d, o):
                def step(b):
                    bk = BANK["q0"][d]
                    if d == 0:
                        pe.wait_ge(self_ok.sem, self_ok.at(b))
                    else:
                        pe.wait_ge(cw_ok.sem, cw_ok.at(b))
                    pe.wait_ge(selfl_ok.sem, selfl_ok.at(b))
                    if first(b):
                        pe.wait_ge(w_low["q0"].sem, w_low["q0"].at(0))
                    product(ps[:, bk, o * S:(o + 1) * S], lambda a, k: w(a, W_Q0 + d * 2 * D, k, D, o * P, (o + 1) * P),
                            lambda a, k: splx[:, a, k, :], range(KC)).then_inc(q0_ps.sem, 1)
                return step

            def k0(b):
                bk = BANK["k0"]
                pe.wait_ge(q0T_ok.sem, q0T_ok.at(b, 1))
                pe.wait_ge(self_ok.sem, self_ok.at(b))
                if first(b):
                    pe.wait_ge(wsm_in.sem, wsm_in.at(0))
                for d in range(2):
                    for o in range(KC):
                        at = (2 * d + o) * KN
                        for k in range(KC):
                            ins = pe.matmul(ps[:, bk, at:at + KN], wsm[:, 0, d, k, o * P:(o + 1) * P], self32[:, k, 0:KN], start=k == 0, stop=k == KC - 1)
                ins.then_inc(k0_ps.sem, 1)

            def affm(c):
                def step(b):
                    if c:
                        pe.wait_ge(am_ok.sem, am_ok.at(b, 1))
                    pe.wait_ge(q0T_ok.sem, q0T_ok.at(b))
                    pe.wait_ge(kblk_ok.sem, kblk_ok.at(b))
                    for d in range(2):
                        for k in range(KC):
                            ins = pe.matmul(ps[:, 3 + d, k * 8 * M:(k + 1) * 8 * M], q0T[:, d, k, c * P:(c + 1) * P],
                                            kblk[:, d, k].rearrange("p h m -> p (h m)"), start=True, stop=True)
                    ins.then_inc(aff_ps.sem, 1)
                return step

            def v0(b):
                bk = BANK["v0"]
                pe.wait_ge(am_ok.sem, am_ok.at(b))
                pe.wait_ge(kvr_ok.sem, kvr_ok.at(b))
                if first(b):
                    pe.wait_ge(wsm_in.sem, wsm_in.at(0))
                for d in range(2):
                    for k in range(KC):
                        ins = pe.matmul(ps[:, bk, d * D:(d + 1) * D], kvr[:, k].rearrange("p r m -> p (r m)"), wsm[:, 1, d, k, :],
                                        start=k == 0, stop=k == KC - 1)
                ins.then_inc(v0_ps.sem, 1)

            def pTt(n):
                def step(b):
                    c, d = divmod(n, 2)
                    bk = BANK["pT"][n % 2]
                    if n == 1:
                        pe.wait_ge(vblk_ok.sem, vblk_ok.at(b))
                    if n >= 2:
                        pe.wait_ge(pT_ok.sem, pT_ok.at(b, n - 1))
                    pe.wait_ge(prob_ok.sem, prob_ok.at(b, c + 1))
                    for g in range(4):
                        at = d * H + 4 * g
                        ins = pe.transpose(ps[:, bk, g * P:(g + 1) * P], prob[:, at:at + 4, :].rearrange("p h m -> p (h m)"), ident)
                    ins.then_inc(pT_ps.sem, 1)
                return step

            def y(b):
                bk = BANK["y"]
                pe.wait_ge(pT_ok.sem, pT_ok.at(b, 3))
                pe.wait_ge(pT_ok.sem, pT_ok.at(b))
                pe.wait_ge(vblk_ok.sem, vblk_ok.at(b))
                for o in range(KC):
                    for d in range(2):
                        for j in range(2):
                            ins = pe.matmul(ps[64 * j:64 * j + 64, bk, o * S:(o + 1) * S], vblk[:, d, 2 * o + j, :], pT[:, d, 2 * o + j, :],
                                            start=d == 0, stop=d == 1)
                ins.then_inc(y_ps.sem, 1)

            def x1T(b):
                bk = BANK["x1"]
                pe.wait_ge(pT_ok.sem, pT_ok.at(b))
                pe.wait_ge(yr_ok.sem, yr_ok.at(b))
                transposes(ps[:, bk], lambda c, k: yT[:, k, c * P:(c + 1) * P], x1_ps)

            def nxT(b):
                bk = BANK["nx"]
                if not first(b):
                    pe.wait_ge(a_ok.sem, a_ok.at(b - 1))
                pe.wait_ge(xr_ok.sem, xr_ok.at(b))
                transposes(ps[:, bk], lambda k, c: xr[:, c, k * P:(k + 1) * P], nx_ps)

            def qk(c):
                def step(b):
                    bk = BANK["qk"][c]
                    if not first(b):
                        pe.wait_ge(at_ok.sem, at_ok.at(b - 1, c + 1))
                    pe.wait_ge(nxl_ok.sem, nxl_ok.at(b))
                    if first(b):
                        pe.wait_ge(w_low["qk"].sem, w_low["qk"].at(0))
                    product(ps[:, bk, :], lambda a, k: sply[:, a, k, c * P:(c + 1) * P], lambda a, k: w(a, W_QK, k, 2 * D, 0, 2 * D),
                            range(KC)).then_inc(qk_ps.sem, 1)
                return step

            def v(c):
                def step(b):
                    bk = BANK["v"]
                    pe.wait_ge(nx_ok.sem, nx_ok.at(b))
                    pe.wait_ge(nxl_ok.sem, nxl_ok.at(b))
                    if first(b):
                        pe.wait_ge(w_low["v"].sem, w_low["v"].at(0))
                    product(ps[:, bk, c * D:(c + 1) * D], lambda a, k: sply[:, a, k, c * P:(c + 1) * P],
                            lambda a, k: w(a, W_V, k, D, 0, D), range(KC)).then_inc(v_ps.sem, 1)
                return step

            def qkT(n):
                def step(b):
                    bk = BANK["qkT"][n]
                    pe.wait_ge(rot_ok.sem, rot_ok.at(b, n + 1))
                    pe.wait_ge(radd_ok.sem, radd_ok.at(b))
                    transposes(ps[:, bk], lambda k, c: t1[:, c, (2 * n + k) * P:(2 * n + k + 1) * P], qkT_ps)
                return step

            def s(h):
                def step(b):
                    bk = h % 2
                    if h < 2:
                        pe.wait_ge(qk_ok.sem, qk_ok.at(b, h + 1))
                    else:
                        pe.wait_ge(mx_ok.sem, mx_ok.at(b, h - 1))
                    if h == 0:
                        pe.wait_ge(stack_in.sem, stack_in.at(b))
                    for c in range(TC):
                        ins = pe.matmul(ps[:, bk, c * S:(c + 1) * S], qst[0:96, h // 2, c * P:(c + 1) * P], kst[0:96, h, :], start=True, stop=True)
                    ins.then_inc(s_ps.sem, 1)
                return step

            def nmT(b):
                bk = BANK["nmT"]
                pe.wait_ge(vv_ok.sem, vv_ok.at(b))
                pe.wait_ge(nm4_ok.sem, nm4_ok.at(b))
                for c in range(TC):
                    ins = pe.transpose(ps[0:4 * PAIRS, bk, c * P:(c + 1) * P],
                                       nm4[:, c].rearrange("p e a q -> p (e a q)").bitcast(FP32), ident)
                ins.then_inc(nmT_ps.sem, 1)

            def st(h):
                def step(b):
                    bk = h % 2
                    if h < 2:
                        pe.wait_ge(mx_ok.sem, mx_ok.at(b, H - 1 + h))
                    else:
                        pe.wait_ge(ex_ok.sem, ex_ok.at(b, h - 1))
                    if h == 0:
                        pe.wait_ge(nrow_in.sem, nrow_in.at(b))
                        if first(b):
                            pe.wait_ge(ones_ok.sem, ones_ok.at(0))
                    for c in range(TC):
                        ins = pe.matmul(ps[:, bk, c * S:(c + 1) * S], kst[0:100, h, c * P:(c + 1) * P], qst[0:100, h // 2, :], start=True, stop=True)
                    ins.then_inc(st_ps.sem, 1)
                return step

            def pv(g):
                def step(b):
                    if g == 0:
                        pe.wait_ge(nrow_ok.sem, nrow_ok.at(b))
                    if g == 2:
                        pe.wait_ge(o_ok.sem, o_ok.at(b, 1))
                    pe.wait_ge(ex_ok.sem, ex_ok.at(b, 4 * g + 4))
                    if g == 0:
                        pe.wait_ge(vv_ok.sem, vv_ok.at(b))
                    for c in range(TC):
                        for j in range(4):
                            h = 4 * g + j
                            ins = pe.matmul(ps[32 * j:32 * j + 32, 2, (g % 2) * S:(g % 2 + 1) * S], vv[:, c, h, :], ex[:, h % EXR, c, :],
                                            start=c == 0, stop=c == TC - 1)
                    ins.then_inc(pv_ps.sem, 1)
                return step

            def oT(c):
                def step(b):
                    bk = BANK["oT"][c]
                    pe.wait_ge(ex_ok.sem, ex_ok.at(b, H - 1 + c))
                    pe.wait_ge(o_ok.sem, o_ok.at(b))
                    for g in range(4):
                        ins = pe.transpose(ps[:, bk, g * P:(g + 1) * P], oT32[:, g, c * P:(c + 1) * P], ident)
                    ins.then_inc(oT_ps.sem, 1)
                return step

            def aT(b):
                bk = BANK["aT"]
                pe.wait_ge(o_ok.sem, o_ok.at(b))
                pe.wait_ge(at_ok.sem, at_ok.at(b))
                transposes(ps[:, bk], lambda k, c: attn[:, c, k * P:(k + 1) * P], aT_ps)

            def wo(c):
                def step(b):
                    bk = BANK["wo"]
                    if not first(b):
                        pe.wait_ge(gelu_ok.sem, gelu_ok.at(b - 1))
                    pe.wait_ge(al_ok.sem, al_ok.at(b))
                    if first(b):
                        pe.wait_ge(w_low["o"].sem, w_low["o"].at(0))
                    product(ps[:, bk, c * D:(c + 1) * D], lambda a, k: spla[:, a, k, c * P:(c + 1) * P],
                            lambda a, k: w(a, W_O, k, D, 0, D), range(KC)).then_inc(wo_ps.sem, 1)
                return step

            def nzTr(b):
                bk = BANK["nz"]
                if not first(b):
                    pe.wait_ge(hm_ok.sem, hm_ok.at(b - 1))
                pe.wait_ge(xr2_ok.sem, xr2_ok.at(b))
                transposes(ps[:, bk], lambda k, c: xr2[:, c, k * P:(k + 1) * P], nz_ps)

            def hidden(name, base, j, i, signal, used, used_before):
                def step(b):
                    bk = BANK[name]
                    if j:
                        pe.wait_ge(used.sem, used.at(b, j))
                    else:
                        pe.wait_ge(used_before.sem, used_before.at(b))
                    pe.wait_ge(nzl_ok.sem, nzl_ok.at(b))
                    if first(b):
                        pe.wait_ge(w_low[name].sem, w_low[name].at(0))
                    n = 2 * j + i
                    product(ps[:, bk, i * S:(i + 1) * S], lambda a, k: w(a, base, k, FF, n * P, (n + 1) * P),
                            lambda a, k: splz[:, a, k, :], range(KC)).then_inc(signal.sem, 1)
                return step

            def down(j, c):
                def step(b):
                    if j == 0 and c == 0 and not first(b):
                        pe.wait_ge(res_ok.sem, res_ok.at(b - 1))
                    pe.wait_ge(hl_ok.sem, hl_ok.at(b, j + 1))
                    if first(b):
                        pe.wait_ge(w_low["d"].sem, w_low["d"].at(0))
                    product(ps[:, 7, c * D:(c + 1) * D], lambda a, i: hs[:, j % 2, a, i, c * P:(c + 1) * P],
                            lambda a, i: w(a, W_D, 2 * j + i, D, 0, D), range(2), first_=j == 0 and c == 0, last_=j == NJ - 1,
                            skip_group_check=True).then_inc(d_ps.sem, 1)
                return step

            def gate(j, i):
                return hidden("g", W_G, j, i, g_ps, gelu_ok, x2_ok)

            def up(j, i):
                return hidden("u", W_U, j, i, u_ps, hm_ok, nz_sb)

            def round_(it):
                step(st(1), it - 1)
                step(pTt(0), it)
                step(st(2), it - 1)
                step(st(3), it - 1)
                step(pTt(1), it)
                step(st(4), it - 1)
                once(cond_1, it)
                step(st(5), it - 1)
                step(pv(0), it - 1)
                step(st(6), it - 1)
                step(st(7), it - 1)
                step(pTt(2), it)
                step(pTt(3), it)
                step(st(8), it - 1)
                step(st(9), it - 1)
                once(cond_q, it + 1)
                step(pv(1), it - 1)
                step(st(10), it - 1)
                step(st(11), it - 1)
                step(y, it)
                step(st(12), it - 1)
                once(cond_2, it)
                step(st(13), it - 1)
                step(pv(2), it - 1)
                step(st(14), it - 1)
                step(st(15), it - 1)
                step(x1T, it)
                step(pv(3), it - 1)
                step(xT, it + 1)
                step(oT(0), it - 1)
                step(oT(1), it - 1)
                step(nzTt, it + 1)
                step(aT, it - 1)
                step(selfm(0), it + 1)
                step(nxT, it)
                step(selfm(1), it + 1)
                step(wo(0), it - 1)
                step(wo(1), it - 1)
                step(adjT, it + 1)
                step(qk(0), it)
                step(qk(1), it)
                step(v(0), it)
                step(q0(0, 0), it + 1)
                step(q0(0, 1), it + 1)
                step(v(1), it)
                step(qkT(0), it)
                step(nzTr, it - 1)
                step(qkT(1), it)
                step(q0(1, 0), it + 1)
                step(k0, it + 1)
                step(q0(1, 1), it + 1)
                step(up(0, 0), it - 1)
                step(gate(0, 0), it - 1)
                step(affm(0), it + 1)
                step(gate(0, 1), it - 1)
                step(up(0, 1), it - 1)
                step(affm(1), it + 1)
                step(gate(1, 0), it - 1)
                step(gate(1, 1), it - 1)
                step(up(1, 0), it - 1)
                step(up(1, 1), it - 1)
                step(gate(2, 0), it - 1)
                step(gate(2, 1), it - 1)
                step(s(0), it)
                step(s(1), it)
                step(up(2, 0), it - 1)
                step(s(2), it)
                step(down(0, 0), it - 1)
                step(s(3), it)
                step(s(4), it)
                step(up(2, 1), it - 1)
                step(s(5), it)
                step(s(6), it)
                step(s(7), it)
                step(down(0, 1), it - 1)
                step(s(8), it)
                step(down(1, 0), it - 1)
                step(s(9), it)
                step(gate(3, 0), it - 1)
                step(s(10), it)
                step(s(11), it)
                step(up(3, 0), it - 1)
                step(s(12), it)
                step(s(13), it)
                step(gate(3, 1), it - 1)
                step(s(14), it)
                step(s(15), it)
                step(up(3, 1), it - 1)
                step(down(1, 1), it - 1)
                step(nmT, it)
                step(v0, it + 1)
                step(down(2, 0), it - 1)
                step(down(2, 1), it - 1)
                step(down(3, 0), it - 1)
                step(down(3, 1), it - 1)
                step(st(0), it)

            rounds(pe, round_, 1, -1)


_IN = ["x", "adj", "condT", "wall", "wsmall", "wcond", "cols", "rows_in", "tabs", "consts"]


def kernel(**inputs):
    import numpy as np
    import concourse.bacc as bacc
    from concourse.bass_utils import run_bass_kernel_spmd

    f = {k: np.asarray(v) for k, v in inputs.items()}

    def rows(a):
        return a.reshape(-1, P, a.shape[1]).transpose(1, 0, 2).reshape(P, -1)

    def column(a):
        return a.reshape(-1, P).T

    def cat(parts):
        return np.ascontiguousarray(np.concatenate(parts, axis=1))

    w_self, wq0, wk0, wout = f["L0_cond_W_self"], f["L0_cond_Wq"], f["L0_cond_Wk"], f["L0_cond_Wout"]
    wqk = np.concatenate([f["L1_cond_wq"], f["L1_cond_wk"]], axis=1)
    bqk = np.concatenate([f["L1_cond_bq"], f["L1_cond_bk"]])
    bqk_swapped = bqk.reshape(-1, 2, DH // 2)[:, ::-1].reshape(-1)
    b2 = [f["L1_cond_t1_b2"], f["L1_cond_t2_b2"]]
    inv_freq = (np.float32(1.0) / np.float32(10000.0) ** (np.arange(0, DH, 2, dtype=np.float32) / np.float32(DH))).astype(np.float32)
    angle = np.arange(S, dtype=np.float32)[:, None] * np.concatenate([inv_freq, inv_freq])[None, :]
    sign = np.where(np.arange(DH) < DH // 2, -1.0, 1.0).astype(np.float32)
    cos, sin = np.cos(angle).astype(np.float32), (np.sin(angle) * sign).astype(np.float32)

    row = np.arange(P)
    eye = np.eye(P, dtype=np.float32)
    j, half, m = np.meshgrid(np.arange(2), np.arange(2), np.arange(M), indexing="ij")
    sel = (row[:, None] == (4 * m + 2 * half + j).reshape(1, -1)).astype(np.float32)
    mask8 = (row[:, None] // DH == np.arange(8)).astype(np.float32)
    mask4 = ((row[:, None] // MP == np.arange(4)) & (row[:, None] % MP < M)).astype(np.float32)
    ones = ((row[:, None] - 96) // 2 == np.arange(H) % 2).astype(np.float32)

    arrays = {
        "x": f["x"],
        "adj": f["mask_BxSxSx11_ik0"],
        "condT": np.ascontiguousarray(rows(f["cond_1024"].T)),
        "wall": cat([rows(w_self[:, :D].T), rows(wq0[0].T), rows(wq0[1].T), rows(wqk), rows(f["L1_cond_wv"]), rows(f["L1_cond_wo"]),
                     rows(f["L1_cond_w_gate"]), rows(f["L1_cond_w_up"]), rows(f["L1_cond_w_down"])]),
        "wsmall": cat([rows(wk0[0].T), rows(wk0[1].T), rows(wout[0].reshape(D, D).T), rows(wout[1].reshape(D, D).T)]),
        "wcond": cat([rows(w_self[:, D:].T), rows(f["L1_cond_t1_w1"]), rows(f["L1_cond_t2_w1"]), rows(f["L1_cond_t1_w2"]), rows(f["L1_cond_t2_w2"])]),
        "cols": cat([column(f["L0_cond_bq"].reshape(-1)), column(f["L0_cond_bk"].reshape(-1)), column(f["L0_cond_bout"].reshape(-1)),
                     column(f["L1_cond_bv"]), column(f["L1_cond_t1_b1"]), column(f["L1_cond_t2_b1"]), column(b2[0]), column(b2[1]),
                     column(f["L1_cond_w_norm1"]), column(f["L1_cond_w_norm2"]), column(bqk), column(bqk_swapped)]),
        "rows_in": cat([f["L1_cond_bo"][None], f["L0_cond_b_self"][None], f["L0_cond_w_bias"][None], f["L0_cond_b_bias"].reshape(1, 1)]),
        "tabs": cat([rows(cos), rows(sin), np.tile(cos.T, (P // DH, 1)), np.tile(sin.T, (P // DH, 1))]),
        "consts": cat([eye, sel, mask8, mask4, ones]),
    }
    nc = bacc.Bacc("TRN2", target_bir_lowering=False, num_devices=1)
    args = [nc.dram_tensor(n, arrays[n].shape, mybir.dt.from_np(arrays[n].dtype), kind="ExternalInput").ap() for n in _IN]
    result = nc.dram_tensor("result", (B, S, D), FP32, kind="ExternalOutput").ap()
    build(nc, *args, result)
    r = run_bass_kernel_spmd(nc, [arrays], core_ids=[0])
    return r.results[0]["result"]
```
